# Optimizing a Trainium2 kernel written in Bass

```python
import numpy as np
import jax
import jax.numpy as jnp

def _softmax(x, axis=-1):
    return jax.nn.softmax(x, axis=axis)

def _gelu(x):
    return jax.nn.gelu(x, approximate=True)

def _silu(x):
    return jax.nn.silu(x)

def _sigmoid(x):
    return jax.nn.sigmoid(x)

def _layernorm(x, axis=-1, eps=1e-05):
    m = jnp.mean(x, axis=axis, keepdims=True)
    v = jnp.var(x, axis=axis, keepdims=True)
    return (x - m) / jnp.sqrt(v + eps)

def _scatter_add(tgt, idx, src, axis=0):
    return tgt.at[idx].add(src)

def _segment_sum(src, seg, n):
    return jax.ops.segment_sum(src, seg, n)
kernel_name = 'mk_recurrent_d2_jaxref_r4_f5de78'

def setup_inputs(seed: int=0):
    np.random.seed(seed)
    _w = jnp.asarray

    def _L0_attn_setup():
        import jax, jax.numpy as jnp
        import numpy as np
        FP32_EPS = 1.1920929e-07

        def rms_norm(x):
            return x * jax.lax.rsqrt(jnp.mean(x * x, axis=-1, keepdims=True) + FP32_EPS)
        key = jax.random.key(seed)
        k1, k2, k3, k4 = jax.random.split(key, 4)
        n_embd, n_qkv = (256, 256)
        B, T = (4, 2048)

        def casted_init(k, out_f, in_f):
            s = 3.0 ** 0.5 * in_f ** (-0.5)
            return jax.random.uniform(k, (out_f, in_f), jnp.float32, -s, s)
        return {'x': jax.random.normal(k1, (B, T, n_embd), jnp.float32), 'w_qkv': casted_init(k2, 3 * n_qkv, n_embd), 'w_swiglu': casted_init(k3, 2 * n_embd, n_qkv), 'w_out': casted_init(k4, n_embd, n_embd)}
    _L0_attn_in = _L0_attn_setup()

    def _L0_ffn_setup():
        import jax, jax.numpy as jnp
        import numpy as np
        import math
        B, S, D = (4, 512, 256)
        E, DFF = (16, 512)
        CAP_FACTOR = 2.0
        ROUTER_HIDDEN = 128
        CAPACITY = int(math.ceil(S * CAP_FACTOR / E))
        key = jax.random.key(seed)
        ks = jax.random.split(key, 6)

        def uinit(k, shape, fan_in):
            bound = math.sqrt(3.0) * math.sqrt(1.0 / 3.0) / math.sqrt(fan_in)
            return jax.random.uniform(k, shape, jnp.float32, -bound, bound)
        return {'hidden_states': jax.random.normal(ks[0], (B, S, D), jnp.float32), 'router_w1': jax.random.normal(ks[1], (D, ROUTER_HIDDEN), jnp.float32) / math.sqrt(D), 'router_w2': jax.random.normal(ks[2], (ROUTER_HIDDEN, E), jnp.float32) / math.sqrt(ROUTER_HIDDEN), 'w1': uinit(ks[3], (E, D, DFF), D), 'w2': uinit(ks[4], (E, D, DFF), D), 'w3': uinit(ks[5], (E, DFF, D), DFF)}
    _L0_ffn_in = _L0_ffn_setup()

    def _L1_attn_setup():
        import jax, jax.numpy as jnp
        import numpy as np
        HIDDEN_DIM = 256
        NUM_HEADS = 16
        LN_EPS = 1e-06

        def _layernorm(x, scale, bias):
            mu = jnp.mean(x, axis=-1, keepdims=True)
            var = jnp.mean(jnp.square(x - mu), axis=-1, keepdims=True)
            return (x - mu) * jax.lax.rsqrt(var + LN_EPS) * scale + bias
        key = jax.random.key(seed)
        ks = jax.random.split(key, 4)
        B, S, D = (2, 512, HIDDEN_DIM)
        x = jax.random.normal(ks[0], (B, S, D), dtype=jnp.float32)
        scale = 1.0 / np.sqrt(D)
        wq = jax.random.normal(ks[1], (D, HIDDEN_DIM), dtype=jnp.float32) * scale
        wk = jax.random.normal(ks[2], (D, HIDDEN_DIM), dtype=jnp.float32) * scale
        wv = jax.random.normal(ks[3], (D, HIDDEN_DIM), dtype=jnp.float32) * scale
        ln_scale = jnp.ones((D,), dtype=jnp.float32)
        ln_bias = jnp.zeros((D,), dtype=jnp.float32)
        return {'x': x, 'ln_scale': ln_scale, 'ln_bias': ln_bias, 'wq': wq, 'wk': wk, 'wv': wv}
    _L1_attn_in = _L1_attn_setup()

    def _L1_ffn_setup():
        import jax, jax.numpy as jnp
        import numpy as np
        B, S, D = (2, 512, 256)
        H = 512
        E = 8
        K = 2
        HS = 512 * 1
        SCALE = 1.0 / float(np.sqrt(D))
        key = jax.random.key(seed)
        ks = jax.random.split(key, 9)
        init = 0.02
        return {'x': jax.random.normal(ks[0], (B, S, D), dtype=jnp.float32), 'Wr': jax.random.normal(ks[1], (D, E), dtype=jnp.float32) * init, 'rb': jnp.zeros((E,), dtype=jnp.float32), 'W1': jax.random.normal(ks[2], (E, D, H), dtype=jnp.float32) * init, 'W2': jax.random.normal(ks[3], (E, H, D), dtype=jnp.float32) * init, 'W3': jax.random.normal(ks[4], (E, D, H), dtype=jnp.float32) * init, 'Ws1': jax.random.normal(ks[5], (D, HS), dtype=jnp.float32) * init, 'Ws2': jax.random.normal(ks[6], (HS, D), dtype=jnp.float32) * init, 'Ws3': jax.random.normal(ks[7], (D, HS), dtype=jnp.float32) * init}
    _L1_ffn_in = _L1_ffn_setup()
    _d = {'L0_attn_x': _L0_attn_in['x'], 'L0_attn_w_qkv': _L0_attn_in['w_qkv'], 'L0_attn_w_swiglu': _L0_attn_in['w_swiglu'], 'L0_attn_w_out': _L0_attn_in['w_out'], 'L0_ffn_router_w1': _L0_ffn_in['router_w1'], 'L0_ffn_router_w2': _L0_ffn_in['router_w2'], 'L0_ffn_w1': _L0_ffn_in['w1'], 'L0_ffn_w2': _L0_ffn_in['w2'], 'L0_ffn_w3': _L0_ffn_in['w3'], 'L1_attn_ln_scale': _L1_attn_in['ln_scale'], 'L1_attn_ln_bias': _L1_attn_in['ln_bias'], 'L1_attn_wq': _L1_attn_in['wq'], 'L1_attn_wk': _L1_attn_in['wk'], 'L1_attn_wv': _L1_attn_in['wv'], 'L1_ffn_Wr': _L1_ffn_in['Wr'], 'L1_ffn_rb': _L1_ffn_in['rb'], 'L1_ffn_W1': _L1_ffn_in['W1'], 'L1_ffn_W2': _L1_ffn_in['W2'], 'L1_ffn_W3': _L1_ffn_in['W3'], 'L1_ffn_Ws1': _L1_ffn_in['Ws1'], 'L1_ffn_Ws2': _L1_ffn_in['Ws2'], 'L1_ffn_Ws3': _L1_ffn_in['Ws3']}
    _x0 = _d['L0_attn_x']
    _d['L0_attn_x'] = jax.random.normal(jax.random.fold_in(jax.random.key(seed), 1), (8, 512, 256), dtype=_x0.dtype)
    del _x0
    return _d

def reference(L0_attn_x, L0_attn_w_qkv, L0_attn_w_swiglu, L0_attn_w_out, L0_ffn_router_w1, L0_ffn_router_w2, L0_ffn_w1, L0_ffn_w2, L0_ffn_w3, L1_attn_ln_scale, L1_attn_ln_bias, L1_attn_wq, L1_attn_wk, L1_attn_wv, L1_ffn_Wr, L1_ffn_rb, L1_ffn_W1, L1_ffn_W2, L1_ffn_W3, L1_ffn_Ws1, L1_ffn_Ws2, L1_ffn_Ws3):

    def _L0_attn_ref(x, w_qkv, w_swiglu, w_out):
        import jax, jax.numpy as jnp
        import numpy as np
        FP32_EPS = 1.1920929e-07

        def rms_norm(x):
            return x * jax.lax.rsqrt(jnp.mean(x * x, axis=-1, keepdims=True) + FP32_EPS)
        qkv = jnp.einsum('btd,ed->bte', rms_norm(x), w_qkv)
        q, k, v = jnp.split(qkv, 3, axis=-1)
        q = rms_norm(q)
        k = rms_norm(k)
        w = jnp.exp(k)
        kv = w * v
        w = jnp.cumsum(w, axis=1)
        kv = jnp.cumsum(kv, axis=1)
        y = kv / (w + 1e-06)
        y = jax.nn.sigmoid(q) * y
        uv = jnp.einsum('bte,fe->btf', y, w_swiglu)
        u, g = jnp.split(uv, 2, axis=-1)
        return x + jnp.einsum('btd,ed->bte', u * jax.nn.silu(g), w_out)

    def _L0_ffn_ref(hidden_states, router_w1, router_w2, w1, w2, w3):
        import jax, jax.numpy as jnp
        import numpy as np
        import math
        B, S, D = (4, 512, 256)
        E, DFF = (16, 512)
        CAP_FACTOR = 2.0
        ROUTER_HIDDEN = 128
        CAPACITY = int(math.ceil(S * CAP_FACTOR / E))
        b, s, d = hidden_states.shape
        e = w1.shape[0]
        cap = CAPACITY
        router_logits = jax.nn.silu(hidden_states @ router_w1) @ router_w2
        expert_probs = jax.nn.softmax(router_logits.transpose(0, 2, 1), axis=-1)
        expert_weights, token_indices = jax.lax.top_k(expert_probs, cap)
        expert_weights = expert_weights / (expert_weights.sum(-1, keepdims=True) + 1e-09)
        expert_inputs = jax.vmap(lambda h, i: h[i])(hidden_states, token_indices)
        gate = jax.nn.silu(jnp.einsum('becd,edf->becf', expert_inputs, w1))
        value = jnp.einsum('becd,edf->becf', expert_inputs, w2)
        expert_out = jnp.einsum('becf,efd->becd', gate * value, w3)
        weighted = expert_out * expert_weights[..., None]

        def combine(idx, vals):
            return jnp.zeros((s, d), vals.dtype).at[idx.reshape(-1)].add(vals.reshape(-1, d))
        output = jax.vmap(combine)(token_indices, weighted)
        return output

    def _L1_attn_ref(x, ln_scale, ln_bias, wq, wk, wv):
        import jax, jax.numpy as jnp
        import numpy as np
        HIDDEN_DIM = 256
        NUM_HEADS = 16
        LN_EPS = 1e-06

        def _layernorm(x, scale, bias):
            mu = jnp.mean(x, axis=-1, keepdims=True)
            var = jnp.mean(jnp.square(x - mu), axis=-1, keepdims=True)
            return (x - mu) * jax.lax.rsqrt(var + LN_EPS) * scale + bias
        bs, sl, fdim = x.shape
        h, hd = (NUM_HEADS, HIDDEN_DIM // NUM_HEADS)
        xn = _layernorm(x, ln_scale, ln_bias)
        q = (xn @ wq).reshape(bs, sl, h, hd).transpose(0, 2, 1, 3)
        k = (xn @ wk).reshape(bs, sl, h, hd).transpose(0, 2, 1, 3)
        v = (xn @ wv).reshape(bs, sl, h, hd).transpose(0, 2, 1, 3)
        scores = jnp.einsum('bhid,bhjd->bhij', q, k)
        probs = jax.nn.softmax(scores / jnp.sqrt(jnp.float32(HIDDEN_DIM)), axis=-1)
        out = jnp.einsum('bhij,bhjd->bhid', probs, v)
        out = out.transpose(0, 2, 1, 3).reshape(bs, sl, -1) + xn
        return out

    def _L1_ffn_ref(x, Wr, rb, W1, W2, W3, Ws1, Ws2, Ws3):
        import jax, jax.numpy as jnp
        import numpy as np
        B, S, D = (2, 512, 256)
        H = 512
        E = 8
        K = 2
        HS = 512 * 1
        SCALE = 1.0 / float(np.sqrt(D))
        logits = jnp.einsum('bsd,de->bse', x, Wr) * SCALE
        _, idx = jax.lax.top_k(logits + rb, K)
        gathered = jnp.take_along_axis(logits, idx, axis=-1)
        w = jax.nn.softmax(gathered, axis=-1)
        w_full = jnp.sum(jax.nn.one_hot(idx, E, dtype=x.dtype) * w[..., None], axis=-2)
        h = jnp.einsum('bsd,edh->bseh', x, W1) * jax.nn.silu(jnp.einsum('bsd,edh->bseh', x, W3))
        expert_out = jnp.einsum('bseh,ehd->bsed', h, W2)
        out = jnp.einsum('bsed,bse->bsd', expert_out, w_full)
        hs = jnp.einsum('bsd,dh->bsh', x, Ws1) * jax.nn.silu(jnp.einsum('bsd,dh->bsh', x, Ws3))
        out = out + jnp.einsum('bsh,hd->bsd', hs, Ws2)
        return out
    x = L0_attn_x
    xn = _layernorm(x, axis=-1)
    s = _L0_attn_ref(xn, L0_attn_w_qkv, L0_attn_w_swiglu, L0_attn_w_out)
    g = _silu(_L0_ffn_ref(xn, L0_ffn_router_w1, L0_ffn_router_w2, L0_ffn_w1, L0_ffn_w2, L0_ffn_w3))
    x = x + s * g
    xn = _layernorm(x, axis=-1)
    s = _L1_attn_ref(xn, L1_attn_ln_scale, L1_attn_ln_bias, L1_attn_wq, L1_attn_wk, L1_attn_wv)
    g = _silu(_L1_ffn_ref(xn, L1_ffn_Wr, L1_ffn_rb, L1_ffn_W1, L1_ffn_W2, L1_ffn_W3, L1_ffn_Ws1, L1_ffn_Ws2, L1_ffn_Ws3))
    x = x + s * g
    return x

_drawn_inputs = setup_inputs


def setup_inputs(seed=0):
    import zlib

    import numpy as np

    out = dict(_drawn_inputs(seed))
    spreads = {'L1_attn_ln_scale': (1.0, 0.2), 'L1_attn_ln_bias': (0.0, 0.1), 'L1_ffn_rb': (0.0, 0.1)}
    factors = {}
    for name, (base, spread) in spreads.items():
        noise = np.random.default_rng([zlib.crc32(name.encode()), seed]).standard_normal(out[name].shape)
        drawn = base * np.exp(spread * noise) if base else spread * noise
        out[name] = jnp.asarray(drawn.astype(out[name].dtype))
    for name, factor in factors.items():
        out[name] = (out[name] * factor).astype(out[name].dtype)
    return out
```

```python
import numpy as np
import concourse.bass as bass
from concourse import mybir
from contextlib import ExitStack

F32 = mybir.dt.float32
F32R = mybir.dt.float32r
I32 = mybir.dt.int32
U32 = mybir.dt.uint32
ALU = mybir.AluOpType
ACT = mybir.ActivationFunctionType
AX = mybir.AxisListType

P = 128
NB, S, D = 8, 512, 256
NTOK = NB * S
T = S // P
DC = D // P
NT = NTOK // P
RH = 128
E0, FF, CAP = 16, 512, 64
FC = FF // P
E1, TOP = 8, 2
GS = 512
NG = (NTOK * TOP + E1 * (GS - 1)) // GS
NH, HD = 16, 16
QH = 4
NQ = NH // QH
LN_EPS, LN1_EPS, RMS_EPS, CUM_EPS = 1e-5, 1e-6, 1.1920929e-07, 1e-6


def at(ap, i):
    names = "abcdef"[: len(ap.shape) - 1]
    inner = " ".join(names[1:])
    return ap[bass.ds(i, 1)].rearrange(f"o {names[0]} {inner} -> (o {names[0]}) {inner}")


def col(ap, i):
    names = "abcdef"[: len(ap.shape) - 2]
    inner = " ".join(names[1:])
    return ap[:, bass.ds(i, 1)].rearrange(f"p o {names[0]} {inner} -> p (o {names[0]}) {inner}")


def land(eng, k):
    eng.sem_inc(k.landed, 1)


class Steps:

    def __init__(self, eng, sem, per_turn, turn):
        self.eng, self.sem, self.per_turn, self.base, self.n = eng, sem, per_turn, turn * per_turn, 0

    def step(self, ins):
        ins.then_inc(self.sem, 1)
        self.n += 1

    def wait(self, back=0):
        self.eng.wait_ge(self.sem, self.base + (self.n - back))

    def end(self):
        assert self.n == self.per_turn, (self.n, self.per_turn)


class Room:

    def __init__(self, nc, ctx, tag):
        self.nc, self.ctx, self.tag = nc, ctx, tag

    def sb(self, name, shape, dt=F32):
        return self.ctx.enter_context(self.nc.sbuf_tensor(self.tag + name, list(shape), dt))

    def banks(self, n):
        return [self.ctx.enter_context(self.nc.psum_tensor(f"{self.tag}bank{i}", [P, 512], F32)) for i in range(n)]

    def sem(self, name):
        return self.ctx.enter_context(self.nc.semaphore(self.tag + name))


def normalise_stats(nc, own, k, x, stats, mean_var):
    land(nc.vector, k)
    for t in range(T):
        own.step(nc.vector.bn_stats(stats[:, t, :], x[:, t, :]))
    own.wait()
    land(nc.vector, k)
    for t in range(T):
        own.step(nc.vector.bn_aggr(mean_var[:, t, :], stats[:, t, :]))


def layer0_mixer(nc, R, k, x_b, xn_b, s0_b, f_b, xs_g, wqkv_d, wsw_d, wout_d, rw1_d, rw2_d):
    sb, sem = R.sb, R.sem
    wqkv, wsw, wout = sb("wqkv", [P, DC, 3 * D]), sb("wsw", [P, DC, 2 * D]), sb("wout", [P, DC, D])
    rw1, rw2 = sb("rw1", [P, DC, RH]), sb("rw2", [P, E0])
    x, xn, xnT = sb("x", [P, T, D]), sb("xn", [P, T, D]), sb("xnT", [P, DC, S])
    stats, mv, veps, rstd = sb("stats", [P, T, 6]), sb("mv", [P, T, 2]), sb("veps", [P, T]), sb("rstd", [P, T])
    half, small = sb("half", [P, 2 * T]), sb("small", [P, 9, 2 * T])
    hT = sb("hT", [P, S])
    qkv, ssq, squares = sb("qkv", [P, T, 3 * D]), sb("ssq", [P, T, 2]), sb("squares", [P, 2, D])
    scale, r2 = sb("scale", [P, T, 2]), sb("r2", [P, T])
    wkv, sums, eq = sb("wkv", [P, T, 2 * D]), sb("sums", [P, 2, 2 * D]), sb("eq", [P, T, D])
    den, rec, y = sb("den", [P, 2, D]), sb("rec", [P, 2, D]), sb("y", [P, T, D])
    tmp = sb("tmp", [P, 2, D])
    yT, sg, guT, xres, s0 = sb("yT", [P, DC, S]), sb("sg", [P, DC, S]), sb("guT", [P, DC, S]), sb("xres", [P, T, D]), sb("s0", [P, T, D])
    B = R.banks(8)

    zeroed = sem("zeroed")
    w_in, x_in, xn_out, xres_in, s0_out = sem("w_in"), sem("x_in"), sem("xn_out"), sem("xres_in"), sem("s0_out")
    veps_done, rstd_done, xn_done = sem("veps_done"), sem("rstd_done"), sem("xn_done")
    xT_ps, xT_sb, h_ps, h_sb, lg_ps, lg_sb = [sem(n) for n in ("xT_ps", "xT_sb", "h_ps", "h_sb", "lg_ps", "lg_sb")]
    qkv_ps, qkv_sb, ssq_done, scale_done = sem("qkv_ps"), sem("qkv_sb"), sem("ssq_done"), sem("scale_done")
    w_done, eq_done, kv_done, sums_done = sem("w_done"), sem("eq_done"), sem("kv_done"), sem("sums_done")
    cum_ps, y_done, yT_ps, yT_sb = sem("cum_ps"), sem("y_done"), sem("yT_ps"), sem("yT_sb")
    uv_ps, sg_done, gu_done, out_ps, s0_done = sem("uv_ps"), sem("sg_done"), sem("gu_done"), sem("out_ps"), sem("s0_done")
    dve1, dve2, pool1, half_set = sem("dve1"), sem("dve2"), sem("pool1"), sem("half_set")

    def turns(eng, turn):
        turn(0, None)
        with eng.Fori(0, NB - 1) as b:
            turn(b + 1, b)
        turn(None, NB - 1)

    with nc.Block() as block:

        @block.sync
        def _(sp):
            for buf, src in ((wqkv, wqkv_d), (wsw, wsw_d), (wout, wout_d), (rw1, rw1_d), (rw2, rw2_d)):
                sp.dma_start(buf[:], src).then_inc(w_in, 16)
            with sp.Fori(0, NB) as b:
                sp.dma_start(at(f_b, b), k.zeros[:].rearrange("p (t d) -> p t d", d=D)).then_inc(zeroed, 16)
            with sp.Fori(0, NG) as g:
                sp.dma_start(at(xs_g, g), k.zeros[:].rearrange("p (t d) -> p t d", d=D)).then_inc(zeroed, 16)

            def turn(n, c):
                if n is not None:
                    sp.wait_ge(xn_done, n)
                    sp.dma_start(x[:], at(x_b, n)).then_inc(x_in, 16)
                if c is not None:
                    sp.wait_ge(xn_out, (c + 1) * 16)
                    sp.wait_ge(s0_done, c)
                    sp.dma_start(xres[:], at(xn_b, c)).then_inc(xres_in, 16)
                if n is not None:
                    sp.wait_ge(xn_done, n + 1)
                    sp.dma_start(at(xn_b, n), xn[:]).then_inc(xn_out, 16)
                if c is not None:
                    sp.wait_ge(s0_done, c + 1)
                    sp.dma_start(at(s0_b, c), s0[:]).then_inc(s0_out, 16)

            turns(sp, turn)
            sp.wait_ge(s0_out, NB * 16)
            sp.wait_ge(zeroed, (NB + NG) * 16)

        @block.tensor
        def _(pe):
            pe.wait_ge(w_in, 5 * 16)

            def turn(n, c):
                if n is not None:
                    pe.wait_ge(xn_done, n + 1)
                    if c is not None:
                        pe.wait_ge(yT_sb, c)
                    for ch in range(DC):
                        for t in range(T):
                            ins = nc.tensor.transpose(B[ch][:, t * P:(t + 1) * P], xn[:, t, ch * P:(ch + 1) * P], k.ident[:])
                    ins.then_inc(xT_ps, 1)
                if c is not None:
                    for t in range(T):
                        bank = B[6 + t % 2]
                        pe.wait_ge(w_done, T * c + t + 1)
                        pe.wait_ge(kv_done, T * c + t + 1)
                        if t == 0:
                            pe.wait_ge(gu_done, DC * c)
                            pe.wait_ge(qkv_sb, T * (c + 1))
                        if t >= 2:
                            pe.wait_ge(y_done, T * c + t - 1)
                            pe.wait_ge(sums_done, 2 * c + t - 1)
                        ins = nc.tensor.matmul(bank[:], k.upper[:], wkv[:, t, :], start=True, stop=t == 0)
                        if t:
                            before = wkv[:, 0, :] if t == 1 else sums[:, t - 2, :]
                            ins = nc.tensor.matmul(bank[:], k.ones[:], before, start=False, stop=True)
                        ins.then_inc(cum_ps, 1)
                if n is not None:
                    pe.wait_ge(xT_sb, n + 1)
                    if c is not None:
                        pe.wait_ge(s0_done, c)
                    for ch in range(DC):
                        ins = nc.tensor.matmul(B[2][:], rw1[:, ch, :], xnT[:, ch, :], start=ch == 0, stop=ch == DC - 1)
                    ins.then_inc(h_ps, 1)
                    for t in range(T):
                        lo, hi = B[4 + 2 * (t % 2)], B[5 + 2 * (t % 2)]
                        if c is not None and t == 0:
                            pe.wait_ge(gu_done, DC * c)
                        if c is not None and t == 1:
                            pe.wait_ge(y_done, T * (c + 1))
                        if t >= 2:
                            pe.wait_ge(qkv_sb, T * n + t - 1)
                        for bank, f0, f1 in ((lo, 0, 2 * D), (hi, 2 * D, 3 * D)):
                            for ch in range(DC):
                                ins = nc.tensor.matmul(bank[:, 0:f1 - f0], xnT[:, ch, t * P:(t + 1) * P], wqkv[:, ch, f0:f1],
                                                       start=ch == 0, stop=ch == DC - 1)
                        ins.then_inc(qkv_ps, 1)
                    pe.wait_ge(h_sb, n + 1)
                    for t in range(T):
                        ins = nc.tensor.matmul(B[3][:, t * E0:(t + 1) * E0], hT[:, t * P:(t + 1) * P], rw2[:], start=True, stop=True)
                    ins.then_inc(lg_ps, 1)
                if c is not None:
                    pe.wait_ge(y_done, T * (c + 1))
                    if n is not None:
                        pe.wait_ge(xT_sb, n + 1)
                    for ch in range(DC):
                        for t in range(T):
                            ins = nc.tensor.transpose(B[ch][:, t * P:(t + 1) * P], y[:, t, ch * P:(ch + 1) * P], k.ident[:])
                    ins.then_inc(yT_ps, 1)
                    pe.wait_ge(yT_sb, c + 1)
                    if n is not None:
                        pe.wait_ge(qkv_sb, T * (n + 1))
                    for j in range(DC):
                        for bank, f in ((B[6 - 2 * j], DC + j), (B[7 - 2 * j], j)):
                            for ch in range(DC):
                                ins = nc.tensor.matmul(bank[:], wsw[:, ch, f * P:(f + 1) * P], yT[:, ch, :], start=ch == 0, stop=ch == DC - 1)
                        ins.then_inc(uv_ps, 1)
                    pe.wait_ge(gu_done, DC * (c + 1))
                    if n is not None:
                        pe.wait_ge(lg_sb, n + 1)
                    for t in range(T):
                        for ch in range(DC):
                            ins = nc.tensor.matmul(B[2 + t // 2][:, (t % 2) * D:(t % 2 + 1) * D], guT[:, ch, t * P:(t + 1) * P],
                                                   wout[:, ch, :], start=ch == 0, stop=ch == DC - 1)
                    ins.then_inc(out_ps, 1)

            turns(pe, turn)

        @block.scalar
        def _(act):
            def turn(n, c):
                if n is not None:
                    act.wait_ge(xT_ps, n + 1)
                    act.wait_ge(lg_ps, n)
                    for ch in range(DC):
                        ins = nc.scalar.activation(xnT[:, ch, :], B[ch][:], ACT.Copy)
                    ins.then_inc(xT_sb, 1)
                    act.wait_ge(h_ps, n + 1)
                    nc.scalar.activation(hT[:], B[2][:], ACT.Silu).then_inc(h_sb, 1)
                    act.wait_ge(scale_done, n)
                    for t in range(T):
                        act.wait_ge(qkv_sb, T * n + t + 1)
                        for i in range(2):
                            act.wait_ge(ssq_done, 2 * (T * n + t))
                            nc.scalar.activation(squares[:, i, :], qkv[:, t, i * D:(i + 1) * D], ACT.Square,
                                                 accum_out=ssq[:, t, i:i + 1]).then_inc(ssq_done, 1)
                if c is not None:
                    act.wait_ge(yT_ps, c + 1)
                    act.wait_ge(out_ps, c)
                    for ch in range(DC):
                        ins = nc.scalar.activation(yT[:, ch, :], B[ch][:], ACT.Copy)
                    ins.then_inc(yT_sb, 1)
                    act.wait_ge(gu_done, DC * c)
                    for j in range(DC):
                        act.wait_ge(uv_ps, DC * c + j + 1)
                        nc.scalar.activation(sg[:, j, :], B[6 - 2 * j][:], ACT.Silu).then_inc(sg_done, 1)
                if n is not None:
                    act.wait_ge(scale_done, n + 1)
                    if c is not None:
                        act.wait_ge(cum_ps, T * (c + 1))
                        act.wait_ge(y_done, T * (c + 1))
                    for t in range(T):
                        nc.scalar.activation(wkv[:, t, 0:D], qkv[:, t, D:2 * D], ACT.Exp, scale=scale[:, t, 1:2]).then_inc(w_done, 1)
                    for t in range(T):
                        nc.scalar.activation(eq[:, t, :], qkv[:, t, 0:D], ACT.Exp, scale=scale[:, t, 0:1]).then_inc(eq_done, 1)

            turns(act, turn)

        @block.gpsimd
        def _(pool):
            nc.gpsimd.memset(half[:], -0.5).then_inc(half_set, 1)
            pool.wait_ge(half_set, 1)

            def turn(n, c):
                if c is not None:
                    pool.wait_ge(w_done, T * (c + 1))
                    pool.wait_ge(kv_done, T * (c + 1))
                    pool.wait_ge(cum_ps, T * c)
                    nc.gpsimd.tensor_tensor(sums[:, 0, :], wkv[:, 0, :], wkv[:, 1, :], ALU.add).then_inc(sums_done, 1)
                    pool.wait_ge(sums_done, 2 * c + 1)
                    nc.gpsimd.tensor_tensor(sums[:, 1, :], sums[:, 0, :], wkv[:, 2, :], ALU.add).then_inc(sums_done, 1)
                if n is None:
                    return
                own = Steps(pool, pool1, 12, n)
                s = [small[:, i, :] for i in range(9)]
                pool.wait_ge(veps_done, n + 1)
                pool.wait_ge(xn_done, n)
                nc.gpsimd.tensor_tensor(rstd[:], veps[:], half[:, 0:T], ALU.pow).then_inc(rstd_done, 1)
                pool.wait_ge(rstd_done, n + 1)
                own.step(nc.gpsimd.tensor_tensor(s[0][:, 0:T], rstd[:], rstd[:], ALU.mult))
                own.wait()
                own.step(nc.gpsimd.tensor_tensor(s[1][:, 0:T], s[0][:, 0:T], mv[:, :, 1], ALU.mult))
                own.wait()
                land(pool, k)
                own.step(nc.gpsimd.tensor_scalar(s[2][:, 0:T], s[1][:, 0:T], RMS_EPS, None, ALU.add))
                own.wait()
                pool.wait_ge(kv_done, T * n)
                own.step(nc.gpsimd.tensor_tensor(r2[:], s[2][:, 0:T], half[:, 0:T], ALU.pow))
                own.wait()
                own.step(nc.gpsimd.tensor_tensor(s[3][:, 0:T], r2[:], r2[:], ALU.mult))
                own.step(nc.gpsimd.tensor_scalar(s[8][:, 0:T], r2[:], -1.0, None, ALU.mult))
                pool.wait_ge(ssq_done, 2 * T * (n + 1))
                land(pool, k)
                own.step(nc.gpsimd.tensor_scalar(s[4], ssq[:].rearrange("p t i -> p (t i)"), 1.0 / D, None, ALU.mult))
                own.wait()
                for i in range(2):
                    own.step(nc.gpsimd.tensor_tensor(s[5].rearrange("p (t i) -> p t i", i=2)[:, :, i],
                                                     s[4].rearrange("p (t i) -> p t i", i=2)[:, :, i], s[3][:, 0:T], ALU.mult))
                own.wait()
                land(pool, k)
                own.step(nc.gpsimd.tensor_scalar(s[6], s[5], RMS_EPS, None, ALU.add))
                own.wait()
                own.step(nc.gpsimd.tensor_tensor(s[7], s[6], half[:], ALU.pow))
                own.wait()
                pool.wait_ge(eq_done, T * n)
                z = s[7].rearrange("p (t i) -> p t i", i=2)
                own.step(nc.gpsimd.tensor_tensor(scale[:, :, 0], z[:, :, 0], s[8][:, 0:T], ALU.mult))
                nc.gpsimd.tensor_tensor(scale[:, :, 1], z[:, :, 1], r2[:], ALU.mult).then_inc(scale_done, 1)
                own.end()

            turns(pool, turn)

        @block.vector
        def _(dve):
            def turn(n, c):
                if n is not None:
                    own = Steps(dve, dve1, 2 * T, n)
                    dve.wait_ge(x_in, 16 * (n + 1))
                    dve.wait_ge(scale_done, n)
                    normalise_stats(nc, own, k, x, stats, mv)
                    own.wait()
                    own.end()
                    nc.vector.tensor_scalar(veps[:], mv[:, :, 1], LN_EPS, None, ALU.add).then_inc(veps_done, 1)
                    dve.wait_ge(rstd_done, n + 1)
                    dve.wait_ge(xn_out, 16 * n)
                    dve.wait_ge(xT_ps, n)
                    for t in range(T):
                        ins = nc.vector.tensor_scalar(xn[:, t, :], x[:, t, :], mv[:, t, 0:1], rstd[:, t:t + 1],
                                                      ALU.subtract, ALU.mult)
                    ins.then_inc(xn_done, 1)
                if c is not None:
                    own = Steps(dve, dve2, 3 * T, c)
                    for t in range(T):
                        bank = B[6 + t % 2]
                        dve.wait_ge(cum_ps, T * c + t + 1)
                        dve.wait_ge(eq_done, T * c + t + 1)
                        own.step(nc.vector.scalar_tensor_tensor(tmp[:, t % 2, :], bank[:, 0:D], CUM_EPS, eq[:, t, :], ALU.add, ALU.mult))
                        own.wait()
                        own.step(nc.vector.scalar_tensor_tensor(den[:, t % 2, :], bank[:, 0:D], CUM_EPS, tmp[:, t % 2, :], ALU.add, ALU.add))
                        own.wait()
                        own.step(nc.vector.reciprocal(rec[:, t % 2, :], den[:, t % 2, :]))
                        own.wait()
                        if t == 0:
                            dve.wait_ge(yT_ps, c)
                        nc.vector.tensor_tensor(y[:, t, :], bank[:, D:2 * D], rec[:, t % 2, :], ALU.mult).then_inc(y_done, 1)
                        dve.wait_ge(y_done, T * c + t + 1)
                    own.end()
                if n is not None:
                    dve.wait_ge(eq_done, T * n)
                    dve.wait_ge(kv_done, T * n)
                    for t in range(T):
                        dve.wait_ge(qkv_ps, T * n + t + 1)
                        nc.vector.tensor_copy(qkv[:, t, 0:2 * D], B[4 + 2 * (t % 2)][:])
                        nc.vector.tensor_copy(qkv[:, t, 2 * D:], B[5 + 2 * (t % 2)][:, 0:D]).then_inc(qkv_sb, 1)
                    dve.wait_ge(lg_ps, n + 1)
                    nc.vector.tensor_copy(k.logits[:, :, bass.ds(n, 1), :].rearrange("p t o e -> p t (o e)"),
                                          B[3][:, 0:T * E0].rearrange("p (t e) -> p t e", e=E0)).then_inc(lg_sb, 1)
                if c is not None:
                    for j in range(DC):
                        dve.wait_ge(uv_ps, DC * c + j + 1)
                        dve.wait_ge(sg_done, DC * c + j + 1)
                        if j == 0:
                            dve.wait_ge(out_ps, c)
                        nc.vector.tensor_tensor(guT[:, j, :], B[7 - 2 * j][:], sg[:, j, :], ALU.mult).then_inc(gu_done, 1)
                    dve.wait_ge(out_ps, c + 1)
                    dve.wait_ge(xres_in, 16 * (c + 1))
                    dve.wait_ge(s0_out, 16 * c)
                    for i in range(2):
                        ins = nc.vector.tensor_tensor(s0[:, 2 * i:2 * i + 2, :].rearrange("p t d -> p (t d)"), B[2 + i][:],
                                                      xres[:, 2 * i:2 * i + 2, :].rearrange("p t d -> p (t d)"), ALU.add)
                    ins.then_inc(s0_done, 1)
                if n is not None:
                    for t in range(T):
                        dve.wait_ge(w_done, T * n + t + 1)
                        nc.vector.scalar_tensor_tensor(wkv[:, t, D:], qkv[:, t, 2 * D:], r2[:, t:t + 1], wkv[:, t, 0:D],
                                                       ALU.mult, ALU.mult).then_inc(kv_done, 1)

            turns(dve, turn)


def choose_tokens(nc, R, k):
    sb, sem = R.sb, R.sem
    BE = NB * E0
    assert BE == P and 2 * CAP == P
    prob, prob2, ex = sb("prob", [P, S]), sb("prob2", [P, S]), sb("ex", [P, S])
    neg_max, total, inv = sb("neg_max", [P, 1]), sb("total", [P, 1]), sb("inv", [P, 1])
    best, place = sb("best", [P, CAP]), sb("place", [P, CAP], U32)
    row0, row0f = sb("row0", [P, 1], I32), sb("row0f", [P, 1])
    rows, share = sb("rows", [P, 2, CAP]), sb("share", [P, 2, CAP])
    wsum, wsum2, winv = sb("wsum", [P, 1]), sb("wsum2", [P, 1]), sb("winv", [P, 1])
    B = R.banks(3)
    row0_done, lgT, exp_done, listed, listedT, own_sem, placed, nm = [sem(n) for n in ("row0_done", "lgT", "exp_done", "listed", "listedT", "dve", "placed", "nm")]
    with nc.Block() as block:

        @block.gpsimd
        def _(pool):
            nc.gpsimd.iota(row0[:], pattern=[[0, 1]], base=0, channel_multiplier=1).then_inc(row0_done, 1)

        @block.tensor
        def _(pe):
            for t in range(T):
                ins = nc.tensor.transpose(B[0][:, t * P:(t + 1) * P], k.logits[:, t].rearrange("p b e -> p (b e)"), k.ident[:])
            ins.then_inc(lgT, 1)
            pe.wait_ge(listed, 1)
            nc.tensor.transpose(B[1][:, 0:P], rows[:].rearrange("p a c -> p (a c)"), k.ident[:])
            nc.tensor.transpose(B[2][:, 0:P], share[:].rearrange("p a c -> p (a c)"), k.ident[:]).then_inc(listedT, 1)

        @block.scalar
        def _(act):
            act.wait_ge(nm, 1)
            nc.scalar.activation(ex[:], B[0][:], ACT.Exp, bias=neg_max[:], accum_out=total[:]).then_inc(exp_done, 1)

        @block.vector
        def _(dve):
            own = Steps(dve, own_sem, 4 + 3 * (CAP // 8) + 7, 0)
            dve.wait_ge(row0_done, 1)
            own.step(nc.vector.tensor_scalar(row0[:], row0[:], 4, 9, ALU.logical_shift_right, ALU.logical_shift_left))
            own.wait()
            own.step(nc.vector.tensor_copy(row0f[:], row0[:]))
            dve.wait_ge(lgT, 1)
            nc.vector.tensor_reduce(neg_max[:], B[0][:], AX.X, ALU.max, negate=True).then_inc(nm, 1)
            dve.wait_ge(exp_done, 1)
            own.step(nc.vector.reciprocal(inv[:], total[:]))
            own.wait()
            own.step(nc.vector.tensor_scalar(prob[:], ex[:], inv[:], None, ALU.mult))
            own.wait()
            src, dst = prob, prob2
            for r in range(CAP // 8):
                eight = best[:, 8 * r:8 * r + 8]
                own.step(nc.vector.max(eight, src[:]))
                own.wait()
                own.step(nc.vector.max_index(place[:, 8 * r:8 * r + 8], eight, src[:]))
                own.step(nc.vector.match_replace(dst[:], eight, src[:], -1.0))
                own.wait()
                src, dst = dst, src
            own.step(nc.vector.tensor_reduce(wsum[:], best[:], AX.X, ALU.add))
            own.wait()
            own.step(nc.vector.tensor_scalar(wsum2[:], wsum[:], 1e-9, None, ALU.add))
            own.wait()
            own.step(nc.vector.reciprocal(winv[:], wsum2[:]))
            own.wait()
            own.step(nc.vector.tensor_scalar(share[:, 0, :], best[:], winv[:], None, ALU.mult))
            own.step(nc.vector.tensor_scalar(share[:, 1, :], best[:], winv[:], None, ALU.mult))
            own.step(nc.vector.tensor_scalar(rows[:, 0, :], place[:], row0f[:], None, ALU.add))
            own.step(nc.vector.tensor_scalar(rows[:, 1, :], place[:], row0f[:], None, ALU.add))
            own.end()
            own.wait()
            nc.vector.tensor_copy(ex[:, 0:1], share[:, 1, 0:1]).then_inc(listed, 1)
            dve.wait_ge(listedT, 1)
            for par in range(2):
                half = slice(par * CAP, (par + 1) * CAP)
                for dst, bank in ((k.slot_row, B[1]), (k.slot_share, B[2])):
                    src = bank[half, 0:P].rearrange("p (t i e) -> p i e t", i=2, e=E0)[:, par]
                    nc.vector.tensor_copy(dst[half], src).then_inc(placed, 1)
            dve.wait_ge(placed, 4)


def layer0_experts(nc, R, k, xn_rows, f_rows, w1_d, w2_d, w3_d):
    sb, sem = R.sb, R.sem
    ST = NB * CAP // P
    w1, w2, w3 = [[sb(f"{n}{u}", s) for u in range(2)] for n, s in (("w1", [P, DC, FF]), ("w2", [P, DC, FF]), ("w3", [P, FC, D]))]
    xg, xgT, sg, hT, y = sb("xg", [P, ST, D]), sb("xgT", [P, DC, S]), sb("sg", [P, 2, S]), sb("hT", [P, FC, S]), sb("y", [P, ST, D])
    slot_a, slot_b = sb("slot_a", [P, ST], U32), sb("slot_b", [P, ST], U32)
    B = R.banks(8)
    slot_a_set, slot_b_set = sem("slot_a_set"), sem("slot_b_set")
    w_in = [sem("w_in0"), sem("w_in1")]
    xg_in, f_out = sem("xg_in"), sem("f_out")
    xT_ps, xT_sb, up_ps, sg_done, h_done, y_ps, y_done = [sem(n) for n in ("xT_ps", "xT_sb", "up_ps", "sg_done", "h_done", "y_ps", "y_done")]

    def turns(eng, turn):
        with eng.Fori(0, E0 // 2 - 1) as j:
            for u in range(2):
                turn(2 * j + u, j, u, False)
        for u in range(2):
            turn(E0 - 2 + u, E0 // 2 - 1, u, u == 1)

    with nc.Block() as block:

        @block.sync
        def _(sp):
            def load(e, u):
                for buf, src in ((w1, w1_d), (w2, w2_d), (w3, w3_d)):
                    sp.dma_start(buf[u][:], at(src, e)).then_inc(w_in[u], 16)

            load(0, 0)
            load(1, 1)
            with sp.Fori(0, E0 // 2 - 1) as j:
                for u in range(2):
                    sp.wait_ge(y_ps, 2 * (2 * j + u + 1))
                    load(2 * j + 2 + u, u)

        @block.gpsimd
        def _(pool):
            def fetch(e):
                nc.gpsimd.tensor_copy(slot_a[:], col(k.slot_row, e)).then_inc(slot_a_set, 1)
                pool.wait_ge(slot_a_set, e + 1)
                land(pool, k)
                for t in range(ST):
                    nc.gpsimd.indirect_dma_start(xg[:, t, :], None, xn_rows, bass.IndirectOffsetOnAxis(slot_a[:, t:t + 1], 0)).then_inc(xg_in, 16)

            def turn(e, j, u, last):
                if not last:
                    pool.wait_ge(xT_ps, e + 1)
                    fetch(e + 1)
                pool.wait_ge(f_out, 16 * ST * e)
                land(pool, k)
                nc.gpsimd.tensor_copy(slot_b[:], col(k.slot_row, e)).then_inc(slot_b_set, 1)
                pool.wait_ge(slot_b_set, e + 1)
                pool.wait_ge(y_done, e + 1)
                land(pool, k)
                for t in range(ST):
                    nc.gpsimd.indirect_dma_start(f_rows, bass.IndirectOffsetOnAxis(slot_b[:, t:t + 1], 0), y[:, t, :], None,
                                                 compute_op=ALU.add).then_inc(f_out, 16)

            fetch(0)
            turns(pool, turn)
            pool.wait_ge(f_out, 16 * ST * E0)

        @block.tensor
        def _(pe):
            def transpose_x(e):
                pe.wait_ge(xg_in, 16 * ST * (e + 1))
                pe.wait_ge(xT_sb, e)
                for c in range(DC):
                    for t in range(ST):
                        ins = nc.tensor.transpose(B[c][:, t * P:(t + 1) * P], xg[:, t, c * P:(c + 1) * P], k.ident[:])
                ins.then_inc(xT_ps, 1)

            def turn(e, j, u, last):
                pe.wait_ge(w_in[u], 3 * 16 * (j + 1))
                pe.wait_ge(xT_sb, e + 1)
                for f in range(FC):
                    gate, value = B[2 + 2 * (f % 2)], B[3 + 2 * (f % 2)]
                    if f >= 2:
                        pe.wait_ge(h_done, FC * e + f - 1)
                    else:
                        pe.wait_ge(h_done, FC * e)
                    for bank, w in ((gate, w1[u]), (value, w2[u])):
                        for c in range(DC):
                            ins = nc.tensor.matmul(bank[:], w[:, c, f * P:(f + 1) * P], xgT[:, c, :], start=c == 0, stop=c == DC - 1)
                    ins.then_inc(up_ps, 1)
                if not last:
                    transpose_x(e + 1)
                pe.wait_ge(h_done, FC * (e + 1))
                pe.wait_ge(y_done, e)
                for t in range(ST):
                    for f in range(FC):
                        ins = nc.tensor.matmul(B[6 + t // 2][:, (t % 2) * D:(t % 2 + 1) * D], hT[:, f, t * P:(t + 1) * P], w3[u][:, f, :],
                                               start=f == 0, stop=f == FC - 1)
                    if t % 2:
                        ins.then_inc(y_ps, 1)

            transpose_x(0)
            turns(pe, turn)

        @block.scalar
        def _(act):
            def copy_xT(e):
                act.wait_ge(xT_ps, e + 1)
                act.wait_ge(up_ps, FC * e)
                for c in range(DC):
                    ins = nc.scalar.activation(xgT[:, c, :], B[c][:], ACT.Copy)
                ins.then_inc(xT_sb, 1)

            def turn(e, j, u, last):
                for f in range(FC):
                    act.wait_ge(up_ps, FC * e + f + 1)
                    act.wait_ge(h_done, FC * e + max(f - 1, 0))
                    nc.scalar.activation(sg[:, f % 2, :], B[2 + 2 * (f % 2)][:], ACT.Silu).then_inc(sg_done, 1)
                if not last:
                    copy_xT(e + 1)

            copy_xT(0)
            turns(act, turn)

        @block.vector
        def _(dve):
            def turn(e, j, u, last):
                for f in range(FC):
                    dve.wait_ge(sg_done, FC * e + f + 1)
                    if f == 0:
                        dve.wait_ge(y_ps, 2 * e)
                    nc.vector.tensor_tensor(hT[:, f, :], B[3 + 2 * (f % 2)][:], sg[:, f % 2, :], ALU.mult).then_inc(h_done, 1)
                dve.wait_ge(f_out, 16 * ST * e)
                for t in range(ST):
                    if t % 2 == 0:
                        dve.wait_ge(y_ps, 2 * e + t // 2 + 1)
                    ins = nc.vector.tensor_scalar(y[:, t, :], B[6 + t // 2][:, (t % 2) * D:(t % 2 + 1) * D],
                                                  col(k.slot_share, e)[:, t:t + 1], None, ALU.mult)
                ins.then_inc(y_done, 1)

            turns(dve, turn)


def layer1_prepare(nc, R, k, x_b, s0_b, f0_b, xn_b, v_b, fs_b, qk_d, w):
    sb, sem = R.sb, R.sem
    wq, wk, wv, wr = sb("wq", [P, DC, D]), sb("wk", [P, DC, D]), sb("wv", [P, DC, D]), sb("wr", [P, DC, E1])
    ws1, ws3, ws2 = sb("ws1", [P, DC, FF]), sb("ws3", [P, DC, FF]), sb("ws2", [P, FC, D])
    lnw, lnb, lnw_row, lnb_row = sb("lnw", [P, DC]), sb("lnb", [P, DC]), sb("lnw_row", [P, D]), sb("lnb_row", [P, D])
    x, s0, f0, g = sb("x", [P, T, D]), sb("s0", [P, T, D]), sb("f0", [P, T, D]), sb("g", [P, T, D])
    stats, mv, veps, rstd = sb("stats", [P, T, 6]), sb("mv", [P, T, 2]), sb("veps", [P, T]), sb("rstd", [P, T])
    half, small, ra = sb("half", [P, T]), sb("small", [P, 3, T]), sb("ra", [P, T])
    xn, xa, xas = sb("xn", [P, T, D]), sb("xa", [P, T, D]), sb("xas", [P, T, D])
    xnT, xaT = sb("xnT", [P, DC, S]), sb("xaT", [P, DC, S])
    hi, lo = sb("hi", [P, 2, S], F32R), sb("lo", [P, 2, S], F32R)
    v = sb("v", [P, T, NH, 2 * HD])
    sg, hT = sb("sg", [P, 2, S]), sb("hT", [P, FC, S])
    B = R.banks(8)
    fs = sb("fs", [P, T, D])
    w_in, x_in, xn_out, v_out, fs_out = sem("w_in"), sem("x_in"), sem("xn_out"), sem("v_out"), sem("fs_out")
    part_out = [sem("part_out0"), sem("part_out1")]
    (g_done, sg0_done, x1_done, veps_done, rstd_done, ra_done, xn_done, xa_done, xas_done, xall_done, tr_ps, tr_sb, lg_ps, lg_sb, v_set, v_ps, v_sb,
     qk_ps, hi_done, lo_done, up_ps, sg_done, h_done, y_ps, y_sb, dve1, pool1, half_set) = [
        sem(n) for n in ("g_done", "sg0_done", "x1_done", "veps_done", "rstd_done", "ra_done", "xn_done", "xa_done", "xas_done", "xall_done", "tr_ps", "tr_sb",
                         "lg_ps", "lg_sb", "v_set", "v_ps", "v_sb", "qk_ps", "hi_done", "lo_done", "up_ps", "sg_done", "h_done", "y_ps",
                         "y_sb", "dve1", "pool1", "half_set")]

    def turns(eng, turn):
        turn(0, None)
        with eng.Fori(0, NB - 1) as b:
            turn(b + 1, b)
        turn(None, NB - 1)

    def flat(ap):
        return ap.rearrange("p t d -> p (t d)")

    with nc.Block() as block:

        @block.sync
        def _(sp):
            loads = [(wq, w["wq"]), (wk, w["wk"]), (wv, w["wv"]), (wr, w["Wr"]), (ws1, w["Ws1"]), (ws3, w["Ws3"]), (ws2, w["Ws2"]),
                     (lnw, w["lnw"]), (lnb, w["lnb"]), (lnw_row, w["lnw_row"]), (lnb_row, w["lnb_row"])]

            def load_x(n):
                for buf, src in ((x, x_b), (s0, s0_b), (f0, f0_b)):
                    sp.dma_start(buf[:], at(src, n)).then_inc(x_in, 16)

            LAST = NB - 1
            load_x(0)
            with nc.allow_non_contiguous_dma(reason="two columns of layer norm weights"):
                for buf, src in loads:
                    sp.dma_start(buf[:], src).then_inc(w_in, 16)

            def turn(n, c):
                if c is not None:
                    for i in range(2 * DC):
                        u = i % 2
                        sp.wait_ge(hi_done, 2 * DC * c + i + 1)
                        sp.dma_start(at(qk_d[i], c), hi[:, u, :].bitcast(F32)).then_inc(part_out[u], 16)
                        sp.wait_ge(lo_done, 2 * DC * c + i + 1)
                        sp.dma_start(at(qk_d[2 * DC + i], c), lo[:, u, :].bitcast(F32)).then_inc(part_out[u], 16)
                    sp.wait_ge(v_sb, T * (c + 1))
                    sp.dma_start(at(v_b, c), v[:].rearrange("p t h d -> p t (h d)")).then_inc(v_out, 16)
                if n is not None:
                    sp.wait_ge(xn_done, n + 1)
                    sp.dma_start(at(xn_b, n), xn[:]).then_inc(xn_out, 16)
                    if not (isinstance(n, int) and n == LAST):
                        load_x(n + 1)
                if c is not None:
                    sp.wait_ge(y_sb, 2 * (c + 1))
                    sp.dma_start(at(fs_b, c), fs[:]).then_inc(fs_out, 16)

            turn(0, None)
            with sp.Fori(0, NB - 2) as b:
                turn(b + 1, b)
            turn(LAST, LAST - 1)
            turn(None, NB - 1)
            sp.wait_ge(xn_out, 16 * NB)
            sp.wait_ge(v_out, 16 * NB)
            sp.wait_ge(fs_out, 16 * NB)
            for u in range(2):
                sp.wait_ge(part_out[u], 4 * 16 * NB)

        @block.tensor
        def _(pe):
            def transposed(src, waits, count):
                pe.wait_ge(*waits)
                pe.wait_ge(tr_sb, count)
                for ch in range(DC):
                    for t in range(T):
                        ins = nc.tensor.transpose(B[ch][:, t * P:(t + 1) * P], src[:, t, ch * P:(ch + 1) * P], k.ident[:])
                ins.then_inc(tr_ps, 1)

            def turn(n, c):
                if c is not None:
                    pe.wait_ge(tr_sb, 2 * (c + 1))
                    pe.wait_ge(y_sb, 2 * c)
                    for t in range(T):
                        for ch in range(DC):
                            ins = nc.tensor.matmul(B[6][:, t * E1:(t + 1) * E1], xnT[:, ch, t * P:(t + 1) * P], wr[:, ch, :],
                                                   start=ch == 0, stop=ch == DC - 1)
                    ins.then_inc(lg_ps, 1)
                    pe.wait_ge(h_done, FC * c)
                    for i in range(2 * DC):
                        for ch in range(DC):
                            ins = nc.tensor.matmul(B[2 + i][:], (wq, wk)[i // DC][:, ch, (i % DC) * P:(i % DC + 1) * P], xaT[:, ch, :],
                                                   start=ch == 0, stop=ch == DC - 1)
                        ins.then_inc(qk_ps, 1)
                    for t in range(T):
                        if t == 1:
                            pe.wait_ge(lg_sb, c + 1)
                        if t >= 2:
                            pe.wait_ge(v_sb, T * c + t - 1)
                        for ch in range(DC):
                            ins = nc.tensor.matmul(B[7 - t % 2][:, 0:D], xaT[:, ch, t * P:(t + 1) * P], wv[:, ch, :],
                                                   start=ch == 0, stop=ch == DC - 1)
                        ins.then_inc(v_ps, 1)
                    for f in range(FC):
                        gate, value = B[2 + 2 * (f % 2)], B[3 + 2 * (f % 2)]
                        if f < 2:
                            pe.wait_ge(lo_done, 2 * DC * c + 2 * f + 2)
                        else:
                            pe.wait_ge(h_done, FC * c + f - 1)
                        for bank, wt in ((gate, ws3), (value, ws1)):
                            for ch in range(DC):
                                ins = nc.tensor.matmul(bank[:], wt[:, ch, f * P:(f + 1) * P], xnT[:, ch, :], start=ch == 0, stop=ch == DC - 1)
                        ins.then_inc(up_ps, 1)
                if n is not None:
                    transposed(xn, (xn_done, n + 1), 2 * n)
                    transposed(xa, (xa_done, n + 1), 2 * n + 1)
                if c is not None:
                    pe.wait_ge(h_done, FC * (c + 1))
                    pe.wait_ge(v_sb, T * (c + 1))
                    for t in range(T):
                        for f in range(FC):
                            ins = nc.tensor.matmul(B[6 + t // 2][:, (t % 2) * D:(t % 2 + 1) * D], hT[:, f, t * P:(t + 1) * P], ws2[:, f, :],
                                                   start=f == 0, stop=f == FC - 1)
                        if t % 2:
                            ins.then_inc(y_ps, 1)

            pe.wait_ge(w_in, 11 * 16)
            turns(pe, turn)

        @block.scalar
        def _(act):
            act.wait_ge(w_in, 11 * 16)

            def turn(n, c):
                if c is not None:
                    for i in range(2 * DC):
                        act.wait_ge(qk_ps, 2 * DC * c + i + 1)
                        act.wait_ge(part_out[i % 2], 2 * 16 * (DC * c + i // 2))
                        nc.scalar.activation(hi[:, i % 2, :], B[2 + i][:], ACT.Copy).then_inc(hi_done, 1)
                if n is not None:
                    act.wait_ge(x_in, 3 * 16 * (n + 1))
                    act.wait_ge(sg0_done, n)
                    nc.scalar.activation(g[:], f0[:], ACT.Silu).then_inc(g_done, 1)
                if c is not None:
                    for f in range(FC):
                        act.wait_ge(up_ps, FC * c + f + 1)
                        act.wait_ge(h_done, FC * c + max(f - 1, 0))
                        nc.scalar.activation(sg[:, f % 2, :], B[2 + 2 * (f % 2)][:], ACT.Silu).then_inc(sg_done, 1)
                if n is not None:
                    act.wait_ge(tr_ps, 2 * n + 1)
                    if c is not None:
                        act.wait_ge(up_ps, FC * (c + 1))
                    for ch in range(DC):
                        ins = nc.scalar.activation(xnT[:, ch, :], B[ch][:], ACT.Copy)
                    ins.then_inc(tr_sb, 1)
                    act.wait_ge(tr_ps, 2 * n + 2)
                    for ch in range(DC):
                        ins = nc.scalar.activation(xaT[:, ch, :], B[ch][:], ACT.Identity, scale=lnw[:, ch:ch + 1], bias=lnb[:, ch:ch + 1])
                    ins.then_inc(tr_sb, 1)

            turns(act, turn)

        @block.gpsimd
        def _(pool):
            nc.gpsimd.memset(v[:, :, :, HD:2 * HD], 0.0).then_inc(v_set, 1)
            nc.gpsimd.memset(half[:], -0.5).then_inc(half_set, 1)
            pool.wait_ge(v_set, 1)
            nc.gpsimd.memset(v[:, :, :, HD:HD + 1], 1.0).then_inc(v_set, 1)
            pool.wait_ge(half_set, 1)
            pool.wait_ge(w_in, 11 * 16)

            def turn(n, c):
                if n is None:
                    return
                own = Steps(pool, pool1, 3, n)
                pool.wait_ge(veps_done, n + 1)
                pool.wait_ge(xn_done, n)
                nc.gpsimd.tensor_tensor(rstd[:], veps[:], half[:], ALU.pow).then_inc(rstd_done, 1)
                pool.wait_ge(rstd_done, n + 1)
                own.step(nc.gpsimd.tensor_tensor(small[:, 0, :], rstd[:], rstd[:], ALU.mult))
                own.wait()
                own.step(nc.gpsimd.tensor_tensor(small[:, 1, :], small[:, 0, :], mv[:, :, 1], ALU.mult))
                own.wait()
                land(pool, k)
                own.step(nc.gpsimd.tensor_scalar(small[:, 2, :], small[:, 1, :], LN1_EPS, None, ALU.add))
                own.wait()
                own.end()
                pool.wait_ge(xa_done, n)
                nc.gpsimd.tensor_tensor(ra[:], small[:, 2, :], half[:], ALU.pow).then_inc(ra_done, 1)
                pool.wait_ge(xa_done, n + 1)
                for t in range(T):
                    ins = nc.gpsimd.tensor_tensor(xas[:, t, :], xa[:, t, :], lnw_row[:], ALU.mult)
                ins.then_inc(xas_done, 1)
                pool.wait_ge(xas_done, n + 1)
                for t in range(T):
                    ins = nc.gpsimd.tensor_tensor(col(k.xa_all, n)[:, t, :], xas[:, t, :], lnb_row[:], ALU.add)
                ins.then_inc(xall_done, 1)

            turns(pool, turn)

        @block.vector
        def _(dve):
            def turn(n, c):
                if c is not None:
                    dve.wait_ge(lg_ps, c + 1)
                    nc.vector.tensor_copy(k.logits1[:, bass.ds(c, 1)].rearrange("p o t e -> p (o t e)"), B[6][:, 0:T * E1]).then_inc(lg_sb, 1)
                    for i in range(2 * DC):
                        dve.wait_ge(hi_done, 2 * DC * c + i + 1)
                        nc.vector.tensor_tensor(lo[:, i % 2, :], B[2 + i][:], hi[:, i % 2, :].bitcast(F32), ALU.subtract).then_inc(lo_done, 1)
                    dve.wait_ge(v_out, 16 * c)
                    for t in range(T):
                        dve.wait_ge(v_ps, T * c + t + 1)
                        nc.vector.tensor_copy(v[:, t, :, 0:HD], B[7 - t % 2][:, 0:D].rearrange("p (h d) -> p h d", d=HD)).then_inc(v_sb, 1)
                if n is not None:
                    own = Steps(dve, dve1, 2 * T, n)
                    x1 = col(k.x1_all, n)
                    dve.wait_ge(g_done, n + 1)
                    nc.vector.tensor_tensor(flat(g[:]), flat(g[:]), flat(s0[:]), ALU.mult).then_inc(sg0_done, 1)
                    dve.wait_ge(sg0_done, n + 1)
                    nc.vector.tensor_tensor(flat(x1), flat(g[:]), flat(x[:]), ALU.add).then_inc(x1_done, 1)
                    dve.wait_ge(x1_done, n + 1)
                    dve.wait_ge(ra_done, n)
                    normalise_stats(nc, own, k, x1, stats, mv)
                    own.wait()
                    own.end()
                    nc.vector.tensor_scalar(veps[:], mv[:, :, 1], LN_EPS, None, ALU.add).then_inc(veps_done, 1)

                def hidden(f):
                    dve.wait_ge(sg_done, FC * c + f + 1)
                    if f == 0:
                        dve.wait_ge(y_ps, 2 * c)
                    nc.vector.tensor_tensor(hT[:, f, :], B[3 + 2 * (f % 2)][:], sg[:, f % 2, :], ALU.mult).then_inc(h_done, 1)

                if c is not None:
                    hidden(0)
                    hidden(1)
                if n is not None:
                    dve.wait_ge(rstd_done, n + 1)
                    dve.wait_ge(xn_out, 16 * n)
                    dve.wait_ge(tr_ps, 2 * n)
                    for t in range(T):
                        ins = nc.vector.tensor_scalar(xn[:, t, :], x1[:, t, :], mv[:, t, 0:1], rstd[:, t:t + 1], ALU.subtract, ALU.mult)
                    ins.then_inc(xn_done, 1)
                    dve.wait_ge(xn_done, n + 1)
                    dve.wait_ge(ra_done, n + 1)
                    dve.wait_ge(xas_done, n)
                    for t in range(T):
                        ins = nc.vector.tensor_scalar(xa[:, t, :], xn[:, t, :], ra[:, t:t + 1], None, ALU.mult)
                    ins.then_inc(xa_done, 1)
                if c is not None:
                    hidden(2)
                    hidden(3)
                    for i in range(2):
                        dve.wait_ge(y_ps, 2 * c + i + 1)
                        if i == 0:
                            dve.wait_ge(fs_out, 16 * c)
                        nc.vector.tensor_copy(flat(fs[:, 2 * i:2 * i + 2, :]), B[6 + i][:]).then_inc(y_sb, 1)

            dve.wait_ge(v_set, 2)
            turns(dve, turn)


def layer1_attention(nc, R, k, qk_v, v_v, o_v, xn_b, xs_rows):
    sb, sem = R.sb, R.sem
    R4, M0 = 4 * HD, 96
    KR = M0 + 2
    qa = [sb(f"qa{i}", [P, QH, S], F32R) for i in range(NQ)]
    ka = [sb(f"ka{i}", [P, QH, S], F32R) for i in range(NQ)]
    va = [sb(f"va{i}", [P, T, QH * 2 * HD]) for i in range(NQ)]
    prob = [sb(f"prob{i}", [P, QH, 2, S]) for i in range(2)]
    neg_max = sb("neg_max", [P, 2, QH * T])
    mh, ml = sb("mh", [QH * T, P], F32R), sb("ml", [QH * T, P], F32R)
    oT, den, o = sb("oT", [P, S]), sb("den", [P, T * QH]), sb("o", [P, T, QH, HD])
    rows, slots = sb("rows", [P, T, D]), sb("slots", [P, TOP, T], U32)
    rows_in, rows_out, slots_set = sem("rows_in"), sem("rows_out"), sem("slots_set")
    B = R.banks(8)
    q_in = [sem(f"q_in{i}") for i in range(NQ)]
    m_in = [sem(f"m_in{i}") for i in range(NQ)]
    set_done, p1_ps, mx_done, mT_ps, mh_done, ml_done, s_ps, p_done, pv_ps, oT_sb, oT_ps, den_done, o_done, o_out = [
        sem(n) for n in ("set_done", "p1_ps", "mx_done", "mT_ps", "mh_done", "ml_done", "s_ps", "p_done", "pv_ps", "oT_sb", "oT_ps",
                         "den_done", "o_done", "o_out")]
    NU = 8

    def batches(eng, first, turn, last):
        first()
        for q in range(NQ):
            turn(0, q, True)
        with eng.Fori(1, NB - 1) as b:
            for q in range(NQ):
                turn(b, q, True)
        for q in range(NQ):
            turn(NB - 1, q, False)
        last()

    def before(b, q):
        if q:
            return b, q - 1
        return None if isinstance(b, int) and b == 0 else (b - 1, NQ - 1)

    def ahead(b, q, d, more):
        if q + d < NQ:
            return b, q + d
        return (b + 1, q + d - NQ) if more else None

    with nc.Block() as block:

        @block.sync
        def _(sp):
            def load(b, q):
                for r in range(4):
                    sp.dma_start(qa[q][r * HD:(r + 1) * HD].bitcast(F32), at(qk_v[r // 2][0][q], b)).then_inc(q_in[q], 16)
                    sp.dma_start(ka[q][r * HD:(r + 1) * HD].bitcast(F32), at(qk_v[r % 2][1][q], b)).then_inc(q_in[q], 16)
                sp.dma_start(va[q][:], at(v_v[q], b)).then_inc(q_in[q], 16)

            def max_rows(b, q):
                g = b * NQ + q
                sp.wait_ge(mh_done, g + 1)
                sp.dma_start(qa[q][M0:M0 + 1].bitcast(F32), mh[:].bitcast(F32)).then_inc(m_in[q], 16)
                sp.wait_ge(ml_done, g + 1)
                sp.dma_start(qa[q][M0 + 1:M0 + 2].bitcast(F32), ml[:].bitcast(F32)).then_inc(m_in[q], 16)

            def first():
                sp.wait_ge(set_done, 2)
                for q in range(NQ):
                    load(0, q)
                max_rows(0, 0)

            def store(b, q):
                sp.wait_ge(o_done, b * NQ + q + 1)
                with nc.allow_non_contiguous_dma(reason="four heads of each row"):
                    sp.dma_start(at(o_v[q], b), o[:].rearrange("p t h d -> p t (h d)")).then_inc(o_out, 16)

            def turn(b, q, more):
                one, prev = ahead(b, q, 1, more), before(b, q)
                if prev and (more or q == 0):
                    sp.wait_ge(pv_ps, 2 * (prev[0] * NQ + prev[1] + 1))
                    load(prev[0] + 1, prev[1])
                if one:
                    max_rows(*one)
                if prev:
                    store(*prev)

            batches(sp, first, turn, lambda: store(NB - 1, NQ - 1))
            sp.wait_ge(o_out, 16 * NB * NQ)

        @block.gpsimd
        def _(pool):
            for i in range(NQ):
                nc.gpsimd.memset(qa[i][64:M0].bitcast(F32), 0.0)
                nc.gpsimd.memset(ka[i][64:M0].bitcast(F32), 0.0)
                ins = nc.gpsimd.memset(ka[i][M0:KR].bitcast(F32), 1.0)
                if i == 0:
                    ins.then_inc(set_done, 1)
            ins.then_inc(set_done, 1)

            pool.wait_ge(set_done, 2)

            with pool.Fori(0, NB) as b:
                pool.dma_start(rows[:], at(xn_b, b)).then_inc(rows_in, 16)
                nc.gpsimd.tensor_copy(slots[:], col(k.slot1, b)).then_inc(slots_set, 1)
                pool.wait_ge(slots_set, b + 1)
                pool.wait_ge(rows_in, 16 * (b + 1))
                land(pool, k)
                for i in range(TOP):
                    for t in range(T):
                        nc.gpsimd.indirect_dma_start(xs_rows, bass.IndirectOffsetOnAxis(slots[:, i, t:t + 1], 0), rows[:, t, :], None).then_inc(rows_out, 16)
                pool.wait_ge(rows_out, TOP * T * 16 * (b + 1))

        @block.tensor
        def _(pe):
            def scores1(g, q, h, t, wait):
                s = g * QH * T + h * T + t
                if wait:
                    pe.wait_ge(mx_done, s - 1)
                nc.tensor.matmul(B[t % 2][:], qa[q][0:M0, h, t * P:(t + 1) * P], ka[q][0:M0, h, :], start=True, stop=True).then_inc(p1_ps, 1)

            def half1(b, q, second, i):
                g = b * NQ + q
                if not second and i == 0:
                    pe.wait_ge(q_in[q], 9 * 16 * (b + 1))
                h = (2 if second else 0) + i // 2
                for t in (2 * (i % 2), 2 * (i % 2) + 1):
                    scores1(g, q, h, t, not (isinstance(g, int) and g == 0 and h == 0 and t < 2))

            def transpose_max(b, q):
                g = b * NQ + q
                pe.wait_ge(mx_done, QH * T * (g + 1))
                if not (isinstance(g, int) and g < 2):
                    pe.wait_ge(o_done, g - 2)
                nc.tensor.transpose(B[7][0:QH * T, 0:P], neg_max[:, q % 2, :], k.ident[:]).then_inc(mT_ps, 1)

            def weigh(b, q, jp):
                g = b * NQ + q
                if jp == 0:
                    pe.wait_ge(oT_sb, g)
                pe.wait_ge(p_done, NU * g + 4 * (jp + 1))
                for jj in range(2):
                    j = 2 * jp + jj
                    for h in range(QH):
                        rows = slice(32 * h, 32 * h + 32)
                        ins = nc.tensor.matmul(B[6][rows, :], va[q][:, j, rows], prob[jp][:, h, jj, :], start=j == 0, stop=j == T - 1,
                                               tile_position=(0, 32 * h))
                ins.then_inc(pv_ps, 1)

            def transpose_o(b, q, one):
                g = b * NQ + q
                pe.wait_ge(oT_sb, g + 1)
                if one:
                    pe.wait_ge(ml_done, g + 3)
                else:
                    pe.wait_ge(o_done, g)
                for t in range(T):
                    ins = nc.tensor.transpose(B[7][:, t * P:(t + 1) * P], oT[:, t * P:(t + 1) * P], k.ident[:])
                ins.then_inc(oT_ps, 1)

            def first():
                pe.wait_ge(set_done, 2)
                for i in range(4):
                    half1(0, 0, False, i)
                for i in range(4):
                    half1(0, 0, True, i)
                transpose_max(0, 0)
                for i in range(4):
                    half1(0, 1, False, i)

            def turn(b, q, more):
                g = b * NQ + q
                one, two, prev = ahead(b, q, 1, more), ahead(b, q, 2, more), before(b, q)
                pe.wait_ge(m_in[q], 2 * 16 * (b + 1))
                for u in range(NU):
                    jp, h = u // QH, u % QH
                    if prev or u > 1:
                        pe.wait_ge(p_done, NU * g + u - 1)
                    for jj in range(2):
                        j = 2 * jp + jj
                        ins = nc.tensor.matmul(B[2 + 2 * (u % 2) + jj][:], ka[q][0:KR, h, j * P:(j + 1) * P], qa[q][0:KR, h, :], start=True, stop=True)
                    ins.then_inc(s_ps, 1)
                    if u < 4 and one:
                        half1(*one, True, u)
                    if u >= 4 and two:
                        half1(*two, False, u - 4)
                    if u == 1 and prev:
                        weigh(*prev, 1)
                    if u == 4 and one:
                        transpose_max(*one)
                    if u == 5:
                        weigh(b, q, 0)
                        if prev:
                            transpose_o(*prev, one)

            def last():
                weigh(NB - 1, NQ - 1, 1)
                transpose_o(NB - 1, NQ - 1, None)

            batches(pe, first, turn, last)

        @block.scalar
        def _(act):
            def copy_o(b, q):
                g = b * NQ + q
                act.wait_ge(pv_ps, 2 * (g + 1))
                act.wait_ge(oT_ps, g)
                nc.scalar.activation(oT[:], B[6][:], ACT.Copy).then_inc(oT_sb, 1)

            def turn(b, q, more):
                g = b * NQ + q
                prev = before(b, q)
                for u in range(NU):
                    jp, h = u // QH, u % QH
                    act.wait_ge(s_ps, NU * g + u + 1)
                    if h == 0 and prev:
                        act.wait_ge(pv_ps, 2 * g + jp - 1)
                    for jj in range(2):
                        ins = nc.scalar.activation(prob[jp][:, h, jj, :], B[2 + 2 * (u % 2) + jj][:], ACT.Exp, scale=float(D) ** -0.5)
                    ins.then_inc(p_done, 1)
                    if u == 3 and prev:
                        copy_o(*prev)

            batches(act, lambda: None, turn, lambda: copy_o(NB - 1, NQ - 1))

        @block.vector
        def _(dve):
            def maxima(b, q, second, i):
                g = b * NQ + q
                h = (2 if second else 0) + i // 2
                for t in (2 * (i % 2), 2 * (i % 2) + 1):
                    s = g * QH * T + h * T + t
                    dve.wait_ge(p1_ps, s + 1)
                    nc.vector.tensor_reduce(neg_max[:, q % 2, h * T + t:h * T + t + 1], B[t % 2][:], AX.X, ALU.max, negate=True).then_inc(mx_done, 1)

            def split_max(b, q):
                g = b * NQ + q
                dve.wait_ge(mT_ps, g + 1)
                if not (isinstance(g, int) and g == 0):
                    pb = (b, q - 1) if q else (b - 1, NQ - 1)
                    dve.wait_ge(m_in[pb[1]], 2 * 16 * (pb[0] + 1))
                nc.vector.tensor_copy(mh[:], B[7][0:QH * T, 0:P]).then_inc(mh_done, 1)
                dve.wait_ge(mh_done, g + 1)
                nc.vector.tensor_tensor(ml[:], B[7][0:QH * T, 0:P], mh[:].bitcast(F32), ALU.subtract).then_inc(ml_done, 1)

            def first():
                for i in range(4):
                    maxima(0, 0, False, i)
                for i in range(4):
                    maxima(0, 0, True, i)
                split_max(0, 0)
                for i in range(4):
                    maxima(0, 1, False, i)

            def divide(b, q):
                g = b * NQ + q
                dve.wait_ge(oT_ps, g + 1)
                v = B[7][:].rearrange("p (t h d) -> p (t h) d", t=T, h=QH)
                nc.vector.reciprocal(den[:], v[:, :, HD]).then_inc(den_done, 1)
                dve.wait_ge(den_done, g + 1)
                dve.wait_ge(o_out, 16 * g)
                nc.vector.tensor_tensor(o[:].rearrange("p t h d -> p (t h) d"), v[:, :, 0:HD],
                                        den[:].unsqueeze(2).broadcast_to([P, T * QH, HD]), ALU.mult).then_inc(o_done, 1)

            def turn(b, q, more):
                one, two, prev = ahead(b, q, 1, more), ahead(b, q, 2, more), before(b, q)
                if one:
                    for i in range(4):
                        maxima(*one, True, i)
                if two:
                    maxima(*two, False, 0)
                if one:
                    split_max(*one)
                if two:
                    maxima(*two, False, 1)
                if prev:
                    divide(*prev)
                if two:
                    maxima(*two, False, 2)
                    maxima(*two, False, 3)

            batches(dve, first, turn, lambda: divide(NB - 1, NQ - 1))


def layer1_route(nc, R, k, rb_row):
    sb, sem = R.sb, R.sem
    assert TOP == 2
    row, scaled, biased = sb("row", [P, E1]), sb("scaled", [P, NT, E1]), sb("biased", [P, NT, E1])
    best, place = sb("best", [P, NT, 8]), sb("place", [P, NT, 8], U32)
    number, numberf = sb("number", [P, E1], I32), sb("numberf", [P, E1])
    group, groupf = sb("group", [P, NG], I32), sb("groupf", [P, NG])
    chosen = sb("chosen", [P, NT, TOP])
    hot = [sb(f"hot{i}", [P, NT, E1]) for i in range(TOP)]
    tmp, both, strict = sb("tmp", [P, NT, E1]), sb("both", [P, NT, E1]), sb("strict", [P, P])
    lg, ex, top, total = sb("lg", [P, TOP, NT]), sb("ex", [P, TOP, NT]), sb("top", [P, NT]), sb("total", [P, NT])
    run = [sb(f"run{i}", [P, NT, E1]) for i in range(2)]
    tile_total = sb("tile_total", [P, NT, E1])
    cnt, cnti, ng, ones8, upto, base = sb("cnt", [P, E1]), sb("cnti", [P, E1], I32), sb("ng", [P, E1]), sb("ones8", [P, E1]), sb("upto", [P, E1]), sb("base", [P, E1])
    past, owner, ownerf, slot = sb("past", [P, NG, E1]), sb("owner", [P, NG]), sb("ownerf", [P, NG]), sb("slot", [P, NT])
    B = R.banks(2)
    made, rb_in, exp_in, exp_done, counted, ranks, own_sem = [sem(n) for n in ("made", "rb_in", "exp_in", "exp_done", "counted", "ranks", "dve")]

    def over(ap, shape, axis):
        return ap.unsqueeze(axis).broadcast_to(shape)

    with nc.Block() as block:

        @block.sync
        def _(sp):
            sp.dma_start(row[:], rb_row).then_inc(rb_in, 16)

        @block.gpsimd
        def _(pool):
            nc.gpsimd.iota(number[:], pattern=[[1, E1]], base=0, channel_multiplier=0).then_inc(made, 1)
            nc.gpsimd.iota(group[:], pattern=[[1, NG]], base=0, channel_multiplier=0).then_inc(made, 1)
            nc.gpsimd.tensor_tensor(strict[:], k.upper[:], k.ident[:], ALU.subtract).then_inc(made, 1)

        @block.tensor
        def _(pe):
            pe.wait_ge(counted, 1)
            flat = both[:].rearrange("p n e -> p (n e)")
            nc.tensor.matmul(B[0][:, 0:NT * E1], strict[:], flat, start=True, stop=True)
            nc.tensor.matmul(B[1][:, 0:NT * E1], k.ones[:], flat, start=True, stop=True).then_inc(ranks, 1)

        @block.scalar
        def _(act):
            act.wait_ge(exp_in, 1)
            nc.scalar.activation(ex[:], lg[:], ACT.Exp).then_inc(exp_done, 1)

        @block.vector
        def _(dve):
            own = Steps(dve, own_sem, 0, 0)

            def do(ins):
                own.step(ins)
                own.wait()

            v = nc.vector
            dve.wait_ge(made, 3)
            dve.wait_ge(rb_in, 16)
            own.step(v.tensor_copy(numberf[:], number[:]))
            own.step(v.tensor_copy(groupf[:], group[:]))
            own.step(v.memset(ones8[:], 1.0))
            do(v.tensor_scalar(scaled[:], k.logits1[:].rearrange("p b t e -> p (b t) e"), float(D) ** -0.5, None, ALU.mult))
            do(v.tensor_tensor(biased[:], scaled[:], over(row[:], [P, NT, E1], 1), ALU.add))
            for n in range(NT):
                own.step(v.max(best[:, n, :], biased[:, n, :]))
            for n in range(NT):
                own.wait(NT - 1)
                own.step(v.max_index(place[:, n, :], best[:, n, :], biased[:, n, :]))
            own.wait()
            do(v.tensor_copy(chosen[:], place[:, :, 0:TOP]))
            for i in range(TOP):
                own.step(v.tensor_tensor(hot[i][:], over(numberf[:], [P, NT, E1], 1), over(chosen[:, :, i], [P, NT, E1], 2), ALU.is_equal))
            own.wait()
            own.n += 0
            v.tensor_tensor(both[:], hot[0][:], hot[1][:], ALU.add).then_inc(counted, 1)
            for i in range(TOP):
                do(v.tensor_tensor(tmp[:], hot[i][:], scaled[:], ALU.mult))
                do(v.tensor_reduce(lg[:, i, :], tmp[:], AX.X, ALU.add))
            do(v.tensor_tensor(top[:], lg[:, 0, :], lg[:, 1, :], ALU.max))
            for i in range(TOP):
                own.step(v.tensor_tensor(lg[:, i, :], lg[:, i, :], top[:], ALU.subtract))
            own.wait()
            v.tensor_copy(k.weight[:, 0, :], lg[:, 0, :]).then_inc(exp_in, 1)
            dve.wait_ge(exp_in, 1)
            dve.wait_ge(exp_done, 1)
            do(v.tensor_tensor(total[:], ex[:, 0, :], ex[:, 1, :], ALU.add))
            do(v.reciprocal(top[:], total[:]))
            for i in range(TOP):
                own.step(v.tensor_tensor(k.weight[:, i, :], ex[:, i, :], top[:], ALU.mult))
            dve.wait_ge(ranks, 1)
            do(v.tensor_copy(tile_total[:].rearrange("p n e -> p (n e)"), B[1][:, 0:NT * E1]))
            src, step, turn = tile_total, 1, 0
            while step < NT:
                dst = run[turn % 2]
                own.step(v.tensor_copy(dst[:, 0:step, :], src[:, 0:step, :]))
                do(v.tensor_tensor(dst[:, step:, :], src[:, step:, :], src[:, 0:NT - step, :], ALU.add))
                src, step, turn = dst, 2 * step, turn + 1
            do(v.tensor_scalar(cnt[:], src[:, NT - 1, :], float(GS - 1), None, ALU.add))
            do(v.tensor_copy(cnti[:], cnt[:]))
            do(v.tensor_scalar(cnti[:], cnti[:], GS.bit_length() - 1, None, ALU.arith_shift_right))
            do(v.tensor_copy(ng[:], cnti[:]))
            do(v.tensor_tensor_scan(upto[:], ones8[:], ng[:], 0.0, ALU.mult, ALU.add))
            do(v.tensor_tensor(base[:], upto[:], ng[:], ALU.subtract))
            do(v.tensor_tensor(past[:], over(upto[:], [P, NG, E1], 1), over(groupf[:], [P, NG, E1], 2), ALU.is_le))
            do(v.tensor_reduce(owner[:], past[:], AX.X, ALU.add))
            do(v.tensor_scalar(ownerf[:], owner[:], float(E1 - 1), None, ALU.min))
            own.step(v.tensor_copy(k.owner[:], ownerf[:]))
            do(v.tensor_scalar(base[:], base[:], float(GS), None, ALU.mult))
            do(v.tensor_tensor(tmp[:], src[:], tile_total[:], ALU.subtract))
            do(v.tensor_tensor(tmp[:].rearrange("p n e -> p (n e)"), B[0][:, 0:NT * E1], tmp[:].rearrange("p n e -> p (n e)"), ALU.add))
            do(v.tensor_tensor(tmp[:], tmp[:], over(base[:], [P, NT, E1], 1), ALU.add))
            for i in range(TOP):
                do(v.tensor_tensor(hot[i][:], hot[i][:], tmp[:], ALU.mult))
                do(v.tensor_reduce(slot[:], hot[i][:], AX.X, ALU.add))
                do(v.tensor_copy(k.slot1[:, :, i, :], slot[:].rearrange("p (b t) -> p b t", t=T)))


def layer1_experts(nc, R, k, xs_g, ys_g, w1_d, w2_d, w3_d):
    sb, sem = R.sb, R.sem
    GT = GS // P
    w1, w3, w2 = [[sb(f"{n}{u}", s) for u in range(2)] for n, s in (("w1", [P, DC, FF]), ("w3", [P, DC, FF]), ("w2", [P, FC, D]))]
    xg, xgT, sg, hT, y = sb("xg", [P, GT, D]), sb("xgT", [P, DC, GS]), sb("sg", [P, 2, GS]), sb("hT", [P, FC, GS]), sb("y", [P, GT, D])
    B = R.banks(8)
    w_in = [sem("w_in0"), sem("w_in1")]
    xg_in, y_out = sem("xg_in"), sem("y_out")
    xT_ps, xT_sb, up_ps, sg_done, h_done, y_ps, y_done = [sem(n) for n in ("xT_ps", "xT_sb", "up_ps", "sg_done", "h_done", "y_ps", "y_done")]
    PAIRS = (NG - 2) // 2

    def turns(eng, turn):
        with eng.Fori(0, PAIRS) as j:
            for u in range(2):
                turn(2 * j + u, j, u)
        for g in range(2 * PAIRS, NG):
            turn(g, g // 2, g % 2)

    def is_last(g, n=1):
        return isinstance(g, int) and g + n >= NG

    with nc.Block() as block:

        @block.sync
        def _(sp):
            def load_weights(g, u):
                e = sp.value_load(k.owner[0:1, bass.ds(g, 1)], min_val=0, max_val=E1 - 1)
                for buf, src in ((w1, w1_d), (w3, w3_d), (w2, w2_d)):
                    sp.dma_start(buf[u][:], at(src, e)).then_inc(w_in[u], 16)

            sp.dma_start(xg[:], at(xs_g, 0)).then_inc(xg_in, 16)
            load_weights(0, 0)
            load_weights(1, 1)

            def turn(g, j, u):
                if not is_last(g):
                    sp.wait_ge(xT_ps, g + 1)
                    sp.dma_start(xg[:], at(xs_g, g + 1)).then_inc(xg_in, 16)
                if not is_last(g, 2):
                    sp.wait_ge(y_ps, 2 * (g + 1))
                    load_weights(g + 2, u)
                sp.wait_ge(y_done, g + 1)
                sp.dma_start(at(ys_g, g), y[:]).then_inc(y_out, 16)

            turns(sp, turn)
            sp.wait_ge(y_out, 16 * NG)

        @block.tensor
        def _(pe):
            def transpose_x(g):
                pe.wait_ge(xg_in, 16 * (g + 1))
                pe.wait_ge(xT_sb, g)
                for c in range(DC):
                    for t in range(GT):
                        ins = nc.tensor.transpose(B[c][:, t * P:(t + 1) * P], xg[:, t, c * P:(c + 1) * P], k.ident[:])
                ins.then_inc(xT_ps, 1)

            def turn(g, j, u):
                pe.wait_ge(w_in[u], 3 * 16 * (j + 1))
                pe.wait_ge(xT_sb, g + 1)
                for f in range(FC):
                    gate, value = B[2 + 2 * (f % 2)], B[3 + 2 * (f % 2)]
                    pe.wait_ge(h_done, FC * g + max(f - 1, 0))
                    for bank, w in ((gate, w3[u]), (value, w1[u])):
                        for c in range(DC):
                            ins = nc.tensor.matmul(bank[:], w[:, c, f * P:(f + 1) * P], xgT[:, c, :], start=c == 0, stop=c == DC - 1)
                    ins.then_inc(up_ps, 1)
                if not is_last(g):
                    transpose_x(g + 1)
                pe.wait_ge(h_done, FC * (g + 1))
                pe.wait_ge(y_done, g)
                for t in range(GT):
                    for f in range(FC):
                        ins = nc.tensor.matmul(B[6 + t // 2][:, (t % 2) * D:(t % 2 + 1) * D], hT[:, f, t * P:(t + 1) * P], w2[u][:, f, :],
                                               start=f == 0, stop=f == FC - 1)
                    if t % 2:
                        ins.then_inc(y_ps, 1)

            transpose_x(0)
            turns(pe, turn)

        @block.scalar
        def _(act):
            def copy_xT(g):
                act.wait_ge(xT_ps, g + 1)
                act.wait_ge(up_ps, FC * g)
                for c in range(DC):
                    ins = nc.scalar.activation(xgT[:, c, :], B[c][:], ACT.Copy)
                ins.then_inc(xT_sb, 1)

            def turn(g, j, u):
                for f in range(FC):
                    act.wait_ge(up_ps, FC * g + f + 1)
                    act.wait_ge(h_done, FC * g + max(f - 1, 0))
                    nc.scalar.activation(sg[:, f % 2, :], B[2 + 2 * (f % 2)][:], ACT.Silu).then_inc(sg_done, 1)
                if not is_last(g):
                    copy_xT(g + 1)

            copy_xT(0)
            turns(act, turn)

        @block.vector
        def _(dve):
            def turn(g, j, u):
                for f in range(FC):
                    dve.wait_ge(sg_done, FC * g + f + 1)
                    if f == 0:
                        dve.wait_ge(y_ps, 2 * g)
                    nc.vector.tensor_tensor(hT[:, f, :], B[3 + 2 * (f % 2)][:], sg[:, f % 2, :], ALU.mult).then_inc(h_done, 1)
                dve.wait_ge(y_out, 16 * g)
                for i in range(2):
                    dve.wait_ge(y_ps, 2 * g + i + 1)
                    ins = nc.vector.tensor_copy(y[:, 2 * i:2 * i + 2, :].rearrange("p t d -> p (t d)"), B[6 + i][:])
                ins.then_inc(y_done, 1)

            turns(dve, turn)


def finish(nc, R, k, ys_rows, fs_b, at_b, out_b):
    sb, sem = R.sb, R.sem
    r = [[sb(f"r{u}{i}", [P, T, D]) for i in range(TOP)] for u in range(2)]
    slots = [sb(f"slots{u}", [P, TOP, T], U32) for u in range(2)]
    fs, ao = [sb(f"fs{u}", [P, T, D]) for u in range(2)], [sb(f"ao{u}", [P, T, D]) for u in range(2)]
    f1, f2, g, s1, s2, y = sb("f1", [P, T, D]), sb("f2", [P, T, D]), sb("g", [P, T, D]), sb("s1", [P, T, D]), sb("s2", [P, T, D]), sb("y", [P, T, D])
    r_in, in_, slots_set = [sem("r_in0"), sem("r_in1")], [sem("in0"), sem("in1")], sem("slots_set")
    f1_done, f2_done, g_done, s1_done, s2_done, y_done, y_out = [sem(n) for n in ("f1_done", "f2_done", "g_done", "s1_done", "s2_done", "y_done", "y_out")]

    def flat(ap):
        return ap.rearrange("p t d -> p (t d)")

    with nc.Block() as block:

        @block.gpsimd
        def _(pool):
            with pool.Fori(0, NB // 2) as j:
                for u in range(2):
                    b = 2 * j + u
                    pool.wait_ge(f2_done, 2 * j)
                    land(pool, k)
                    nc.gpsimd.tensor_copy(slots[u][:], col(k.slot1, b)).then_inc(slots_set, 1)
                    pool.wait_ge(slots_set, b + 1)
                    land(pool, k)
                    for i in range(TOP):
                        for t in range(T):
                            nc.gpsimd.indirect_dma_start(r[u][i][:, t, :], None, ys_rows,
                                                         bass.IndirectOffsetOnAxis(slots[u][:, i, t:t + 1], 0)).then_inc(r_in[u], 16)

        @block.sync
        def _(sp):
            for u in range(2):
                sp.dma_start(fs[u][:], at(fs_b, u)).then_inc(in_[u], 16)
                sp.dma_start(ao[u][:], at(at_b, u)).then_inc(in_[u], 16)

            def turn(b, u, more):
                sp.wait_ge(y_done, b + 1)
                sp.dma_start(at(out_b, b), y[:]).then_inc(y_out, 16)
                if more:
                    sp.dma_start(fs[u][:], at(fs_b, b + 2)).then_inc(in_[u], 16)
                    sp.dma_start(ao[u][:], at(at_b, b + 2)).then_inc(in_[u], 16)

            with sp.Fori(0, NB // 2 - 1) as j:
                for u in range(2):
                    turn(2 * j + u, u, True)
            for u in range(2):
                turn(NB - 2 + u, u, False)
            sp.wait_ge(y_out, 16 * NB)

        @block.scalar
        def _(act):
            with act.Fori(0, NB) as b:
                act.wait_ge(f2_done, b + 1)
                act.wait_ge(s2_done, b)
                nc.scalar.activation(g[:], f2[:], ACT.Silu).then_inc(g_done, 1)

        @block.vector
        def _(dve):
            with dve.Fori(0, NB // 2) as j:
                for u in range(2):
                    b = 2 * j + u
                    dve.wait_ge(in_[u], 2 * 16 * (j + 1))
                    dve.wait_ge(r_in[u], TOP * T * 16 * (j + 1))
                    w = [k.weight[:, i, :].rearrange("p (b t) -> p b t", t=T)[:, bass.ds(b, 1)].rearrange("p o t -> p (o t)") for i in range(TOP)]
                    for t in range(T):
                        nc.vector.scalar_tensor_tensor(f1[:, t, :], r[u][0][:, t, :], w[0][:, t:t + 1], fs[u][:, t, :], ALU.mult, ALU.add).then_inc(f1_done, 1)
                    dve.wait_ge(f1_done, T * (b + 1))
                    dve.wait_ge(g_done, b)
                    for t in range(T):
                        ins = nc.vector.scalar_tensor_tensor(f2[:, t, :], r[u][1][:, t, :], w[1][:, t:t + 1], f1[:, t, :], ALU.mult, ALU.add)
                    ins.then_inc(f2_done, 1)
                    nc.vector.tensor_tensor(flat(s1[:]), flat(ao[u][:]), flat(col(k.xa_all, b)), ALU.add).then_inc(s1_done, 1)
                    dve.wait_ge(s1_done, b + 1)
                    dve.wait_ge(g_done, b + 1)
                    nc.vector.tensor_tensor(flat(s2[:]), flat(s1[:]), flat(g[:]), ALU.mult).then_inc(s2_done, 1)
                    dve.wait_ge(s2_done, b + 1)
                    dve.wait_ge(y_out, 16 * b)
                    nc.vector.tensor_tensor(flat(y[:]), flat(s2[:]), flat(col(k.x1_all, b)), ALU.add).then_inc(y_done, 1)


class Constants:
    pass


def constants(nc, R, k):
    k.ident, k.ones, k.upper = R.sb("ident", [P, P]), R.sb("ones", [P, P]), R.sb("upper", [P, P])
    k.landed = R.sem("landed")
    k.zeros = R.sb("zeros", [P, T * D])
    k.logits = R.sb("logits", [P, T, NB, E0])
    k.slot_row, k.slot_share = R.sb("slot_row", [P, E0, NB * CAP // P], U32), R.sb("slot_share", [P, E0, NB * CAP // P])
    k.x1_all, k.xa_all = [R.sb(n, [P, NB, T, D]) for n in ("x1_all", "xa_all")]
    k.weight, k.slot1, k.owner = R.sb("weight", [P, TOP, NT]), R.sb("slot1", [P, NB, TOP, T], U32), R.sb("owner", [P, NG], I32)
    k.logits1 = R.sb("logits1", [P, NB, T, E1])
    k.made = made = R.sem("made")
    with nc.Block() as block:

        @block.gpsimd
        def _(pool):
            nc.gpsimd.memset(k.zeros[:], 0.0).then_inc(made, 1)
            nc.gpsimd.memset(k.ones[:], 1.0).then_inc(made, 1)
            nc.gpsimd.memset(k.ident[:], 0.0).then_inc(made, 1)
            pool.wait_ge(made, 3)
            nc.gpsimd.affine_select(out=k.ident[:], in_=k.ident[:], compare_op=ALU.not_equal, fill=1.0,
                                    base=0, pattern=[[-1, P]], channel_multiplier=1).then_inc(made, 1)
            nc.gpsimd.affine_select(out=k.upper[:], in_=k.ones[:], compare_op=ALU.is_ge, fill=0.0,
                                    base=0, pattern=[[1, P]], channel_multiplier=-1).then_inc(made, 1)
            pool.wait_ge(made, 5)


def build(nc, a, out, phases=9):
    def scratch(name, shape, dt=F32):
        return nc.dram_tensor(name, list(shape), dt).ap()

    def tiled(ap):
        return ap.rearrange("(b t p) d -> b p t d", t=T, p=P)

    def chunked(ap):
        return ap.rearrange("(c p) f -> p c f", p=P)

    x = a["x"].rearrange("b s d -> (b s) d")
    xn0, s0, f0 = scratch("xn0", [NTOK, D]), scratch("s0", [NTOK, D]), scratch("f0", [NTOK, D])
    fs1, at1 = scratch("fs1", [NTOK, D]), scratch("at1", [NTOK, D])
    xn1, v1 = scratch("xn1", [NTOK, D]), scratch("v1", [NTOK, NH * 2 * HD])
    qk1 = scratch("qk1", [4 * DC, P, NTOK])
    xs, ys = scratch("xs", [NG * GS, D]), scratch("ys", [NG * GS, D])
    k = Constants()
    with ExitStack() as whole:
        constants(nc, Room(nc, whole, "c_"), k)
        with ExitStack() as ctx:
            layer0_mixer(nc, Room(nc, ctx, "m0_"), k, tiled(x), tiled(xn0), tiled(s0), tiled(f0), tiled(xs), chunked(a["w_qkv"]), chunked(a["w_swiglu"]),
                         chunked(a["w_out"]), chunked(a["router_w1"]), a["router_w2"])
        if phases < 2:
            return
        with ExitStack() as ctx:
            choose_tokens(nc, Room(nc, ctx, "ct_"), k)
        with ExitStack() as ctx:
            layer0_experts(nc, Room(nc, ctx, "e0_"), k, xn0, f0, a["w1"].rearrange("e (c p) f -> e p c f", p=P),
                           a["w2"].rearrange("e (c p) f -> e p c f", p=P), a["w3"].rearrange("e (c p) f -> e p c f", p=P))
        if phases < 3:
            return
        lnw, lnb = a["ln_scale"], a["ln_bias"]
        weights = {n: chunked(a[n]) for n in ("wq", "wk", "wv", "Wr", "Ws1", "Ws3", "Ws2")}
        weights.update(lnw=lnw.rearrange("(c p) -> p c", p=P), lnb=lnb.rearrange("(c p) -> p c", p=P),
                       lnw_row=lnw.partition_broadcast(P), lnb_row=lnb.partition_broadcast(P))
        with ExitStack() as ctx:
            layer1_prepare(nc, Room(nc, ctx, "p1_"), k, tiled(x), tiled(s0), tiled(f0), tiled(xn1), tiled(v1), tiled(fs1),
                           [qk1[i].rearrange("p (b s) -> b p s", s=S) for i in range(4 * DC)], weights)
        if phases < 4:
            return
        parts = qk1.rearrange("(l a c) p n -> l a (c p) n", l=2, a=2)
        qk_v = [[[parts[l, i, q * QH * HD:(q + 1) * QH * HD].rearrange("(h d) (b s) -> b d h s", d=HD, s=S) for q in range(NQ)]
                 for i in range(2)] for l in range(2)]
        v_v = [tiled(v1[:, q * QH * 2 * HD:(q + 1) * QH * 2 * HD]) for q in range(NQ)]
        o_v = [tiled(at1[:, q * QH * HD:(q + 1) * QH * HD]) for q in range(NQ)]
        with ExitStack() as ctx:
            layer1_route(nc, Room(nc, ctx, "r1_"), k, a["rb"].partition_broadcast(P))
        with ExitStack() as ctx:
            layer1_attention(nc, Room(nc, ctx, "a1_"), k, qk_v, v_v, o_v, tiled(xn1), xs)
        if phases < 5:
            return
        with ExitStack() as ctx:
            layer1_experts(nc, Room(nc, ctx, "e1_"), k, tiled(xs), tiled(ys), a["W1"].rearrange("e (c p) f -> e p c f", p=P),
                           a["W2"].rearrange("e (c p) f -> e p c f", p=P), a["W3"].rearrange("e (c p) f -> e p c f", p=P))
        with ExitStack() as ctx:
            finish(nc, Room(nc, ctx, "f_"), k, ys, tiled(fs1), tiled(at1), tiled(out.rearrange("b s d -> (b s) d")))


_NAMES = ["x", "w_qkv", "w_swiglu", "w_out", "router_w1", "router_w2", "w1", "w2", "w3", "ln_scale", "ln_bias", "wq", "wk", "wv",
          "Wr", "rb", "W1", "W2", "W3", "Ws1", "Ws2", "Ws3"]


def layout(inputs):
    full = {n.split("_", 2)[2]: v for n, v in inputs.items()}
    arrays = {n: np.ascontiguousarray(full[n]) for n in _NAMES}
    for n in ("w_qkv", "w_swiglu", "w_out"):
        arrays[n] = np.ascontiguousarray(np.asarray(full[n]).T)
    return arrays


def kernel(**inputs):
    import concourse.bacc as _bacc
    from concourse.bass_utils import run_bass_kernel_spmd as _run

    nc = _bacc.Bacc("TRN2", target_bir_lowering=False, num_devices=1)
    arrays = layout(inputs)
    a = {n: nc.dram_tensor("in_" + n, v.shape, mybir.dt.from_np(v.dtype), kind="ExternalInput").ap() for n, v in arrays.items()}
    out = nc.dram_tensor("out", (NB, S, D), F32, kind="ExternalOutput").ap()
    build(nc, a, out)
    r = _run(nc, [{"in_" + n: v for n, v in arrays.items()}], core_ids=[0])
    return r.results[0]["out"]
```

```python
import numpy as np
import concourse.bass as bass
from concourse import mybir
from contextlib import ExitStack

F32 = mybir.dt.float32
F32R = mybir.dt.float32r
I32 = mybir.dt.int32
U32 = mybir.dt.uint32
ALU = mybir.AluOpType
ACT = mybir.ActivationFunctionType
AX = mybir.AxisListType

P = 128
NB, S, D = 8, 512, 256
NTOK = NB * S
T = S // P
DC = D // P
NT = NTOK // P
RH = 128
E0, FF, CAP = 16, 512, 64
FC = FF // P
E1, TOP = 8, 2
GS = 512
NG = (NTOK * TOP + E1 * (GS - 1)) // GS
NH, HD = 16, 16
QH = 4
NQ = NH // QH
ROW = D + 2
LN_EPS, LN1_EPS, RMS_EPS, CUM_EPS = 1e-5, 1e-6, 1.1920929e-07, 1e-6


def at(ap, i):
    names = "abcdef"[: len(ap.shape) - 1]
    inner = " ".join(names[1:])
    return ap[bass.ds(i, 1)].rearrange(f"o {names[0]} {inner} -> (o {names[0]}) {inner}")


def col(ap, i):
    names = "abcdef"[: len(ap.shape) - 2]
    inner = " ".join(names[1:])
    return ap[:, bass.ds(i, 1)].rearrange(f"p o {names[0]} {inner} -> p (o {names[0]}) {inner}")


def land(eng, k):
    eng.sem_inc(k.landed, 1)


class Steps:

    def __init__(self, eng, sem, per_turn, turn):
        self.eng, self.sem, self.per_turn, self.base, self.n = eng, sem, per_turn, turn * per_turn, 0

    def step(self, ins):
        ins.then_inc(self.sem, 1)
        self.n += 1

    def wait(self, back=0):
        self.eng.wait_ge(self.sem, self.base + (self.n - back))

    def end(self):
        assert self.n == self.per_turn, (self.n, self.per_turn)


class Room:

    def __init__(self, nc, ctx, tag):
        self.nc, self.ctx, self.tag = nc, ctx, tag

    def sb(self, name, shape, dt=F32):
        return self.ctx.enter_context(self.nc.sbuf_tensor(self.tag + name, list(shape), dt))

    def banks(self, n):
        return [self.ctx.enter_context(self.nc.psum_tensor(f"{self.tag}bank{i}", [P, 512], F32)) for i in range(n)]

    def sem(self, name):
        return self.ctx.enter_context(self.nc.semaphore(self.tag + name))


def product3(nc, out, a, b, pairs, first=True, last=True):
    for n, (x, y) in enumerate(pairs):
        for m, (i, l) in enumerate(((0, 0), (0, 1), (1, 0))):
            ins = nc.tensor.matmul(out, a[i][x], b[l][y], start=first and n == m == 0, stop=last and n == len(pairs) - 1 and m == 2)
    return ins


def normalise_stats(nc, own, k, x, stats, mean_var):
    land(nc.vector, k)
    for t in range(T):
        own.step(nc.vector.bn_stats(stats[:, t, :], x[:, t, :]))
    own.wait()
    land(nc.vector, k)
    for t in range(T):
        own.step(nc.vector.bn_aggr(mean_var[:, t, :], stats[:, t, :]))


def layer0_mixer(nc, R, k, x_b, xn_b, s0_b, f_b, xs_g, none_rows, wqkv_d, wsw_d, wout_d, rw1_d, rw2_d):
    sb, sem = R.sb, R.sem
    wqkv, wsw, wout = sb("wqkv", [P, DC, 3 * D]), sb("wsw", [P, DC, 2 * D]), sb("wout", [P, DC, D])
    rw1, rw2 = sb("rw1", [P, DC, RH]), sb("rw2", [P, E0])
    x, xn, xnT = sb("x", [P, T, D]), sb("xn", [P, T, D]), sb("xnT", [P, DC, S])
    stats, mv, veps, rstd = sb("stats", [P, T, 6]), sb("mv", [P, T, 2]), sb("veps", [P, T]), sb("rstd", [P, T])
    half, small = sb("half", [P, 2 * T]), sb("small", [P, 9, 2 * T])
    hT = sb("hT", [P, S])
    qkv, ssq, squares = sb("qkv", [P, T, 3 * D]), sb("ssq", [P, T, 2]), sb("squares", [P, 2, D])
    scale, r2 = sb("scale", [P, T, 2]), sb("r2", [P, T])
    wkv, sums, eq = sb("wkv", [P, T, 2 * D]), sb("sums", [P, 2, 2 * D]), sb("eq", [P, T, D])
    den, rec, y = sb("den", [P, 2, D]), sb("rec", [P, 2, D]), sb("y", [P, T, D])
    tmp = sb("tmp", [P, 2, D])
    yT, sg, guT, xres, s0 = sb("yT", [P, DC, S]), sb("sg", [P, DC, S]), sb("guT", [P, DC, S]), sb("xres", [P, T, D]), sb("s0", [P, T, D])
    B = R.banks(8)

    zeroed = sem("zeroed")
    w_in, x_in, xn_out, xres_in, s0_out = sem("w_in"), sem("x_in"), sem("xn_out"), sem("xres_in"), sem("s0_out")
    veps_done, rstd_done, xn_done = sem("veps_done"), sem("rstd_done"), sem("xn_done")
    xT_ps, xT_sb, h_ps, h_sb, lg_ps, lg_sb = [sem(n) for n in ("xT_ps", "xT_sb", "h_ps", "h_sb", "lg_ps", "lg_sb")]
    qkv_ps, qkv_sb, ssq_done, scale_done = sem("qkv_ps"), sem("qkv_sb"), sem("ssq_done"), sem("scale_done")
    w_done, eq_done, kv_done, sums_done = sem("w_done"), sem("eq_done"), sem("kv_done"), sem("sums_done")
    cum_ps, y_done, yT_ps, yT_sb = sem("cum_ps"), sem("y_done"), sem("yT_ps"), sem("yT_sb")
    uv_ps, sg_done, gu_done, out_ps, s0_done = sem("uv_ps"), sem("sg_done"), sem("gu_done"), sem("out_ps"), sem("s0_done")
    dve1, dve2, pool1, half_set = sem("dve1"), sem("dve2"), sem("pool1"), sem("half_set")

    def turns(eng, turn):
        turn(0, None)
        with eng.Fori(0, NB - 1) as b:
            turn(b + 1, b)
        turn(None, NB - 1)

    with nc.Block() as block:

        @block.sync
        def _(sp):
            def load_weights():
                for buf, src in ((rw1, rw1_d), (wqkv, wqkv_d), (rw2, rw2_d), (wsw, wsw_d), (wout, wout_d)):
                    sp.dma_start(buf[:], src).then_inc(w_in, 16)

            def zero(c):
                sp.dma_start(at(f_b, c), k.zeros[:].rearrange("p (t d) -> p t d", d=D)).then_inc(zeroed, 16)
                each = -(-NG // NB)
                for i in range(each):
                    if not isinstance(c, int) or each * c + i < NG:
                        sp.dma_start(at(xs_g, each * c + i), k.pad[:]).then_inc(zeroed, 16)

            def turn(n, c):
                if n is not None:
                    sp.wait_ge(xn_done, n)
                    sp.dma_start(x[:], at(x_b, n)).then_inc(x_in, 16)
                if c is None:
                    load_weights()
                if c is not None:
                    sp.wait_ge(xn_out, (c + 1) * 16)
                    sp.wait_ge(s0_done, c)
                    sp.dma_start(xres[:], at(xn_b, c)).then_inc(xres_in, 16)
                    zero(c)
                if n is not None:
                    sp.wait_ge(xn_done, n + 1)
                    sp.dma_start(at(xn_b, n), xn[:]).then_inc(xn_out, 16)
                if c is not None:
                    sp.wait_ge(s0_done, c + 1)
                    sp.dma_start(at(s0_b, c), s0[:]).then_inc(s0_out, 16)

            sp.dma_start(none_rows, k.zeros[:].rearrange("p (t d) -> p t d", d=D)).then_inc(zeroed, 16)
            turns(sp, turn)
            sp.wait_ge(s0_out, NB * 16)
            sp.wait_ge(zeroed, (NB + NG + 1) * 16)

        @block.tensor
        def _(pe):
            def turn(n, c):
                if n is not None:
                    pe.wait_ge(xn_done, n + 1)
                    if c is not None:
                        pe.wait_ge(yT_sb, c)
                    for ch in range(DC):
                        for t in range(T):
                            ins = nc.tensor.transpose(B[ch][:, t * P:(t + 1) * P], xn[:, t, ch * P:(ch + 1) * P], k.ident[:])
                    ins.then_inc(xT_ps, 1)
                if c is not None:
                    for t in range(T):
                        bank = B[6 + t % 2]
                        pe.wait_ge(w_done, T * c + t + 1)
                        pe.wait_ge(kv_done, T * c + t + 1)
                        if t == 0:
                            pe.wait_ge(gu_done, DC * c)
                            pe.wait_ge(qkv_sb, T * (c + 1))
                        if t >= 2:
                            pe.wait_ge(y_done, T * c + t - 1)
                            pe.wait_ge(sums_done, 2 * c + t - 1)
                        ins = nc.tensor.matmul(bank[:], k.upper[:], wkv[:, t, :], start=True, stop=t == 0)
                        if t:
                            before = wkv[:, 0, :] if t == 1 else sums[:, t - 2, :]
                            ins = nc.tensor.matmul(bank[:], k.ones[:], before, start=False, stop=True)
                        ins.then_inc(cum_ps, 1)
                if n is not None:
                    pe.wait_ge(xT_sb, n + 1)
                    pe.wait_ge(w_in, 5 * 16)
                    if c is not None:
                        pe.wait_ge(s0_done, c)
                    for ch in range(DC):
                        ins = nc.tensor.matmul(B[2][:], rw1[:, ch, :], xnT[:, ch, :], start=ch == 0, stop=ch == DC - 1)
                    ins.then_inc(h_ps, 1)
                    for t in range(T):
                        lo, hi = B[4 + 2 * (t % 2)], B[5 + 2 * (t % 2)]
                        if c is not None and t == 0:
                            pe.wait_ge(gu_done, DC * c)
                        if c is not None and t == 1:
                            pe.wait_ge(y_done, T * (c + 1))
                        if t >= 2:
                            pe.wait_ge(qkv_sb, T * n + t - 1)
                        for bank, f0, f1 in ((lo, 0, 2 * D), (hi, 2 * D, 3 * D)):
                            for ch in range(DC):
                                ins = nc.tensor.matmul(bank[:, 0:f1 - f0], xnT[:, ch, t * P:(t + 1) * P], wqkv[:, ch, f0:f1],
                                                       start=ch == 0, stop=ch == DC - 1)
                        ins.then_inc(qkv_ps, 1)
                    pe.wait_ge(h_sb, n + 1)
                    for t in range(T):
                        ins = nc.tensor.matmul(B[3][:, t * E0:(t + 1) * E0], hT[:, t * P:(t + 1) * P], rw2[:], start=True, stop=True)
                    ins.then_inc(lg_ps, 1)
                if c is not None:
                    pe.wait_ge(y_done, T * (c + 1))
                    if n is not None:
                        pe.wait_ge(xT_sb, n + 1)
                    for ch in range(DC):
                        for t in range(T):
                            ins = nc.tensor.transpose(B[ch][:, t * P:(t + 1) * P], y[:, t, ch * P:(ch + 1) * P], k.ident[:])
                    ins.then_inc(yT_ps, 1)
                    pe.wait_ge(yT_sb, c + 1)
                    if n is not None:
                        pe.wait_ge(qkv_sb, T * (n + 1))
                    for j in range(DC):
                        for bank, f in ((B[6 - 2 * j], DC + j), (B[7 - 2 * j], j)):
                            for ch in range(DC):
                                ins = nc.tensor.matmul(bank[:], wsw[:, ch, f * P:(f + 1) * P], yT[:, ch, :], start=ch == 0, stop=ch == DC - 1)
                        ins.then_inc(uv_ps, 1)
                    pe.wait_ge(gu_done, DC * (c + 1))
                    if n is not None:
                        pe.wait_ge(lg_sb, n + 1)
                    for t in range(T):
                        for ch in range(DC):
                            ins = nc.tensor.matmul(B[2 + t // 2][:, (t % 2) * D:(t % 2 + 1) * D], guT[:, ch, t * P:(t + 1) * P],
                                                   wout[:, ch, :], start=ch == 0, stop=ch == DC - 1)
                    ins.then_inc(out_ps, 1)

            turns(pe, turn)

        @block.scalar
        def _(act):
            def turn(n, c):
                if n is not None:
                    act.wait_ge(xT_ps, n + 1)
                    act.wait_ge(lg_ps, n)
                    for ch in range(DC):
                        ins = nc.scalar.activation(xnT[:, ch, :], B[ch][:], ACT.Copy)
                    ins.then_inc(xT_sb, 1)
                    act.wait_ge(h_ps, n + 1)
                    nc.scalar.activation(hT[:], B[2][:], ACT.Silu).then_inc(h_sb, 1)
                    act.wait_ge(scale_done, n)
                    for t in range(T):
                        act.wait_ge(qkv_sb, T * n + t + 1)
                        for i in range(2):
                            act.wait_ge(ssq_done, 2 * (T * n + t))
                            nc.scalar.activation(squares[:, i, :], qkv[:, t, i * D:(i + 1) * D], ACT.Square,
                                                 accum_out=ssq[:, t, i:i + 1]).then_inc(ssq_done, 1)
                if c is not None:
                    act.wait_ge(yT_ps, c + 1)
                    act.wait_ge(out_ps, c)
                    for ch in range(DC):
                        ins = nc.scalar.activation(yT[:, ch, :], B[ch][:], ACT.Copy)
                    ins.then_inc(yT_sb, 1)
                    act.wait_ge(gu_done, DC * c)
                    for j in range(DC):
                        act.wait_ge(uv_ps, DC * c + j + 1)
                        nc.scalar.activation(sg[:, j, :], B[6 - 2 * j][:], ACT.Silu).then_inc(sg_done, 1)
                if n is not None:
                    act.wait_ge(scale_done, n + 1)
                    if c is not None:
                        act.wait_ge(cum_ps, T * (c + 1))
                        act.wait_ge(y_done, T * (c + 1))
                    for t in range(T):
                        nc.scalar.activation(wkv[:, t, 0:D], qkv[:, t, D:2 * D], ACT.Exp, scale=scale[:, t, 1:2]).then_inc(w_done, 1)
                    for t in range(T):
                        nc.scalar.activation(eq[:, t, :], qkv[:, t, 0:D], ACT.Exp, scale=scale[:, t, 0:1]).then_inc(eq_done, 1)

            turns(act, turn)

        @block.gpsimd
        def _(pool):
            nc.gpsimd.memset(half[:], -0.5).then_inc(half_set, 1)
            pool.wait_ge(half_set, 1)

            def turn(n, c):
                if c is not None:
                    pool.wait_ge(w_done, T * (c + 1))
                    pool.wait_ge(kv_done, T * (c + 1))
                    pool.wait_ge(cum_ps, T * c)
                    nc.gpsimd.tensor_tensor(sums[:, 0, :], wkv[:, 0, :], wkv[:, 1, :], ALU.add).then_inc(sums_done, 1)
                    pool.wait_ge(sums_done, 2 * c + 1)
                    nc.gpsimd.tensor_tensor(sums[:, 1, :], sums[:, 0, :], wkv[:, 2, :], ALU.add).then_inc(sums_done, 1)
                if n is None:
                    return
                own = Steps(pool, pool1, 12, n)
                s = [small[:, i, :] for i in range(9)]
                pool.wait_ge(veps_done, n + 1)
                pool.wait_ge(xn_done, n)
                nc.gpsimd.tensor_tensor(rstd[:], veps[:], half[:, 0:T], ALU.pow).then_inc(rstd_done, 1)
                pool.wait_ge(rstd_done, n + 1)
                own.step(nc.gpsimd.tensor_tensor(s[0][:, 0:T], rstd[:], rstd[:], ALU.mult))
                own.wait()
                own.step(nc.gpsimd.tensor_tensor(s[1][:, 0:T], s[0][:, 0:T], mv[:, :, 1], ALU.mult))
                own.wait()
                land(pool, k)
                own.step(nc.gpsimd.tensor_scalar(s[2][:, 0:T], s[1][:, 0:T], RMS_EPS, None, ALU.add))
                own.wait()
                pool.wait_ge(kv_done, T * n)
                own.step(nc.gpsimd.tensor_tensor(r2[:], s[2][:, 0:T], half[:, 0:T], ALU.pow))
                own.wait()
                own.step(nc.gpsimd.tensor_tensor(s[3][:, 0:T], r2[:], r2[:], ALU.mult))
                own.step(nc.gpsimd.tensor_scalar(s[8][:, 0:T], r2[:], -1.0, None, ALU.mult))
                pool.wait_ge(ssq_done, 2 * T * (n + 1))
                land(pool, k)
                own.step(nc.gpsimd.tensor_scalar(s[4], ssq[:].rearrange("p t i -> p (t i)"), 1.0 / D, None, ALU.mult))
                own.wait()
                for i in range(2):
                    own.step(nc.gpsimd.tensor_tensor(s[5].rearrange("p (t i) -> p t i", i=2)[:, :, i],
                                                     s[4].rearrange("p (t i) -> p t i", i=2)[:, :, i], s[3][:, 0:T], ALU.mult))
                own.wait()
                land(pool, k)
                own.step(nc.gpsimd.tensor_scalar(s[6], s[5], RMS_EPS, None, ALU.add))
                own.wait()
                own.step(nc.gpsimd.tensor_tensor(s[7], s[6], half[:], ALU.pow))
                own.wait()
                pool.wait_ge(eq_done, T * n)
                z = s[7].rearrange("p (t i) -> p t i", i=2)
                own.step(nc.gpsimd.tensor_tensor(scale[:, :, 0], z[:, :, 0], s[8][:, 0:T], ALU.mult))
                nc.gpsimd.tensor_tensor(scale[:, :, 1], z[:, :, 1], r2[:], ALU.mult).then_inc(scale_done, 1)
                own.end()

            turns(pool, turn)

        @block.vector
        def _(dve):
            def turn(n, c):
                if n is not None:
                    own = Steps(dve, dve1, 2 * T, n)
                    dve.wait_ge(x_in, 16 * (n + 1))
                    dve.wait_ge(scale_done, n)
                    normalise_stats(nc, own, k, x, stats, mv)
                    own.wait()
                    own.end()
                    nc.vector.tensor_scalar(veps[:], mv[:, :, 1], LN_EPS, None, ALU.add).then_inc(veps_done, 1)
                    dve.wait_ge(rstd_done, n + 1)
                    dve.wait_ge(xn_out, 16 * n)
                    dve.wait_ge(xT_ps, n)
                    for t in range(T):
                        ins = nc.vector.tensor_scalar(xn[:, t, :], x[:, t, :], mv[:, t, 0:1], rstd[:, t:t + 1],
                                                      ALU.subtract, ALU.mult)
                    ins.then_inc(xn_done, 1)
                if c is not None:
                    own = Steps(dve, dve2, 3 * T, c)
                    for t in range(T):
                        bank = B[6 + t % 2]
                        dve.wait_ge(cum_ps, T * c + t + 1)
                        dve.wait_ge(eq_done, T * c + t + 1)
                        own.step(nc.vector.scalar_tensor_tensor(tmp[:, t % 2, :], bank[:, 0:D], CUM_EPS, eq[:, t, :], ALU.add, ALU.mult))
                        own.wait()
                        own.step(nc.vector.scalar_tensor_tensor(den[:, t % 2, :], bank[:, 0:D], CUM_EPS, tmp[:, t % 2, :], ALU.add, ALU.add))
                        own.wait()
                        own.step(nc.vector.reciprocal(rec[:, t % 2, :], den[:, t % 2, :]))
                        own.wait()
                        if t == 0:
                            dve.wait_ge(yT_ps, c)
                        nc.vector.tensor_tensor(y[:, t, :], bank[:, D:2 * D], rec[:, t % 2, :], ALU.mult).then_inc(y_done, 1)
                        dve.wait_ge(y_done, T * c + t + 1)
                    own.end()
                if n is not None:
                    dve.wait_ge(eq_done, T * n)
                    dve.wait_ge(kv_done, T * n)
                    for t in range(T):
                        dve.wait_ge(qkv_ps, T * n + t + 1)
                        nc.vector.tensor_copy(qkv[:, t, 0:2 * D], B[4 + 2 * (t % 2)][:])
                        nc.vector.tensor_copy(qkv[:, t, 2 * D:], B[5 + 2 * (t % 2)][:, 0:D]).then_inc(qkv_sb, 1)
                    dve.wait_ge(lg_ps, n + 1)
                    nc.vector.tensor_copy(k.logits[:, :, bass.ds(n, 1), :].rearrange("p t o e -> p t (o e)"),
                                          B[3][:, 0:T * E0].rearrange("p (t e) -> p t e", e=E0)).then_inc(lg_sb, 1)
                if c is not None:
                    for j in range(DC):
                        dve.wait_ge(uv_ps, DC * c + j + 1)
                        dve.wait_ge(sg_done, DC * c + j + 1)
                        if j == 0:
                            dve.wait_ge(out_ps, c)
                        nc.vector.tensor_tensor(guT[:, j, :], B[7 - 2 * j][:], sg[:, j, :], ALU.mult).then_inc(gu_done, 1)
                    dve.wait_ge(out_ps, c + 1)
                    dve.wait_ge(xres_in, 16 * (c + 1))
                    dve.wait_ge(s0_out, 16 * c)
                    for i in range(2):
                        ins = nc.vector.tensor_tensor(s0[:, 2 * i:2 * i + 2, :].rearrange("p t d -> p (t d)"), B[2 + i][:],
                                                      xres[:, 2 * i:2 * i + 2, :].rearrange("p t d -> p (t d)"), ALU.add)
                    ins.then_inc(s0_done, 1)
                if n is not None:
                    for t in range(T):
                        dve.wait_ge(w_done, T * n + t + 1)
                        nc.vector.scalar_tensor_tensor(wkv[:, t, D:], qkv[:, t, 2 * D:], r2[:, t:t + 1], wkv[:, t, 0:D],
                                                       ALU.mult, ALU.mult).then_inc(kv_done, 1)

            turns(dve, turn)


def choose_tokens(nc, R, k):
    sb, sem = R.sb, R.sem
    BE = NB * E0
    assert BE == P and 2 * CAP == P
    prob, prob2, ex = sb("prob", [P, S]), sb("prob2", [P, S]), sb("ex", [P, S])
    neg_max, total, inv = sb("neg_max", [P, 1]), sb("total", [P, 1]), sb("inv", [P, 1])
    best, place = sb("best", [P, CAP]), sb("place", [P, CAP], U32)
    row0, row0f = sb("row0", [P, 1], I32), sb("row0f", [P, 1])
    rows, share = sb("rows", [P, 2, CAP]), sb("share", [P, 2, CAP])
    wsum, wsum2, winv = sb("wsum", [P, 1]), sb("wsum2", [P, 1]), sb("winv", [P, 1])
    B = R.banks(3)
    row0_done, lgT, exp_done, listed, listedT, own_sem, placed, nm = [sem(n) for n in ("row0_done", "lgT", "exp_done", "listed", "listedT", "dve", "placed", "nm")]
    with nc.Block() as block:

        @block.gpsimd
        def _(pool):
            nc.gpsimd.iota(row0[:], pattern=[[0, 1]], base=0, channel_multiplier=1).then_inc(row0_done, 1)

        @block.tensor
        def _(pe):
            for t in range(T):
                ins = nc.tensor.transpose(B[0][:, t * P:(t + 1) * P], k.logits[:, t].rearrange("p b e -> p (b e)"), k.ident[:])
            ins.then_inc(lgT, 1)
            pe.wait_ge(listed, 1)
            nc.tensor.transpose(B[1][:, 0:P], rows[:].rearrange("p a c -> p (a c)"), k.ident[:])
            nc.tensor.transpose(B[2][:, 0:P], share[:].rearrange("p a c -> p (a c)"), k.ident[:]).then_inc(listedT, 1)

        @block.scalar
        def _(act):
            act.wait_ge(nm, 1)
            nc.scalar.activation(ex[:], B[0][:], ACT.Exp, bias=neg_max[:], accum_out=total[:]).then_inc(exp_done, 1)

        @block.vector
        def _(dve):
            own = Steps(dve, own_sem, 4 + 3 * (CAP // 8) + 6, 0)
            dve.wait_ge(row0_done, 1)
            own.step(nc.vector.tensor_scalar(row0[:], row0[:], 4, 9, ALU.logical_shift_right, ALU.logical_shift_left))
            own.wait()
            own.step(nc.vector.tensor_copy(row0f[:], row0[:]))
            dve.wait_ge(lgT, 1)
            nc.vector.tensor_reduce(neg_max[:], B[0][:], AX.X, ALU.max, negate=True).then_inc(nm, 1)
            dve.wait_ge(exp_done, 1)
            own.step(nc.vector.reciprocal(inv[:], total[:]))
            own.wait()
            own.step(nc.vector.tensor_scalar(prob[:], ex[:], inv[:], None, ALU.mult))
            own.wait()
            src, dst = prob, prob2
            for r in range(CAP // 8):
                eight = best[:, 8 * r:8 * r + 8]
                own.step(nc.vector.max(eight, src[:]))
                own.wait()
                own.step(nc.vector.max_index(place[:, 8 * r:8 * r + 8], eight, src[:]))
                own.step(nc.vector.match_replace(dst[:], eight, src[:], -1.0))
                own.wait()
                src, dst = dst, src
            own.step(nc.vector.tensor_reduce(wsum[:], best[:], AX.X, ALU.add))
            own.wait()
            own.step(nc.vector.tensor_scalar(wsum2[:], wsum[:], 1e-9, None, ALU.add))
            own.wait()
            own.step(nc.vector.reciprocal(winv[:], wsum2[:]))
            own.wait()
            own.step(nc.vector.tensor_scalar(share[:, 0, :], best[:], winv[:], None, ALU.mult))
            own.step(nc.vector.tensor_scalar(share[:, 1, :], best[:], winv[:], None, ALU.mult))
            own.step(nc.vector.tensor_scalar(rows[:, 0, :], place[:], row0f[:], None, ALU.add))
            nc.vector.tensor_scalar(rows[:, 1, :], place[:], row0f[:], None, ALU.add).then_inc(listed, 1)
            own.end()
            dve.wait_ge(listedT, 1)
            for par in range(2):
                half = slice(par * CAP, (par + 1) * CAP)
                for dst, bank in ((k.slot_row, B[1]), (k.slot_share, B[2])):
                    src = bank[half, 0:P].rearrange("p (t i e) -> p i e t", i=2, e=E0)[:, par]
                    nc.vector.tensor_copy(dst[half], src).then_inc(placed, 1)
            dve.wait_ge(placed, 4)


def layer0_experts(nc, R, k, xn_rows, f_rows, w1_d, w2_d, w3_d):
    sb, sem = R.sb, R.sem
    ST = NB * CAP // P
    YP = ST // 2
    raw = [sb(f"raw{i}", s) for i, s in enumerate(([P, DC, FF], [P, DC, FF], [P, FC, D]))]
    w1, w2, w3 = [[[sb(f"{n}{u}{part}", s, F32R) for part in ("hi", "lo")] for u in range(2)] for n, s in (("w1", [P, DC, FF]), ("w2", [P, DC, FF]), ("w3", [P, FC, D]))]
    xT, hT = [[sb(n + part, s, F32R) for part in ("hi", "lo")] for n, s in (("xT", [P, DC, S]), ("hT", [P, FC, S]))]
    h = sb("h", [P, 2, S])
    xg, sg, y = sb("xg", [P, ST, D]), sb("sg", [P, 2, S]), sb("y", [P, ST, D])
    slot_a, slot_b = sb("slot_a", [P, ST], U32), sb("slot_b", [P, ST], U32)
    B = R.banks(8)
    slot_a_set, slot_b_set = sem("slot_a_set"), sem("slot_b_set")
    w_in = sem("w_in")
    xg_in, f_out = sem("xg_in"), sem("f_out")
    xT_ps, x_hi, x_lo, w_hi, w_lo, up_ps, sg_done, h_done, h_hi, h_lo, y_ps, y_done = [
        sem(n) for n in ("xT_ps", "x_hi", "x_lo", "w_hi", "w_lo", "up_ps", "sg_done", "h_done", "h_hi", "h_lo", "y_ps", "y_done")]

    def turns(eng, turn):
        with eng.Fori(0, E0 // 2 - 1) as j:
            for u in range(2):
                turn(2 * j + u, j, u, False)
        for u in range(2):
            turn(E0 - 2 + u, E0 // 2 - 1, u, u == 1)

    with nc.Block() as block:

        @block.sync
        def _(sp):
            def load(e):
                for buf, src in zip(raw, (w1_d, w2_d, w3_d)):
                    sp.dma_start(buf[:], at(src, e)).then_inc(w_in, 16)

            load(0)
            with sp.Fori(1, E0) as e:
                sp.wait_ge(w_lo, 3 * e)
                load(e)

        @block.gpsimd
        def _(pool):
            def fetch(e):
                nc.gpsimd.tensor_copy(slot_a[:], col(k.slot_row, e)).then_inc(slot_a_set, 1)
                pool.wait_ge(slot_a_set, e + 1)
                land(pool, k)
                for t in range(ST):
                    nc.gpsimd.indirect_dma_start(xg[:, t, :], None, xn_rows, bass.IndirectOffsetOnAxis(slot_a[:, t:t + 1], 0)).then_inc(xg_in, 16)

            def turn(e, j, u, last):
                if not last:
                    pool.wait_ge(xT_ps, e + 1)
                    fetch(e + 1)
                pool.wait_ge(f_out, 16 * ST * e)
                land(pool, k)
                nc.gpsimd.tensor_copy(slot_b[:], col(k.slot_row, e)).then_inc(slot_b_set, 1)
                pool.wait_ge(slot_b_set, e + 1)
                pool.wait_ge(y_done, e + 1)
                land(pool, k)
                for t in range(ST):
                    nc.gpsimd.indirect_dma_start(f_rows, bass.IndirectOffsetOnAxis(slot_b[:, t:t + 1], 0), y[:, t, :], None,
                                                 compute_op=ALU.add).then_inc(f_out, 16)

            fetch(0)
            turns(pool, turn)
            pool.wait_ge(f_out, 16 * ST * E0)

        @block.tensor
        def _(pe):
            def transpose_x(e):
                pe.wait_ge(xg_in, 16 * ST * (e + 1))
                pe.wait_ge(x_lo, e)
                for c in range(DC):
                    for t in range(ST):
                        ins = nc.tensor.transpose(B[c][:, t * P:(t + 1) * P], xg[:, t, c * P:(c + 1) * P], k.ident[:])
                ins.then_inc(xT_ps, 1)

            def turn(e, j, u, last):
                pe.wait_ge(w_lo, 3 * (e + 1))
                pe.wait_ge(x_lo, e + 1)
                for f in range(FC):
                    gate, value = B[2 + 2 * (f % 2)], B[3 + 2 * (f % 2)]
                    pe.wait_ge(h_done, FC * e + max(f - 1, 0))
                    for bank, w in ((gate, w1), (value, w2)):
                        ins = product3(nc, bank[:, 0:S], w[u], xT, [((slice(None), c, slice(f * P, (f + 1) * P)), (slice(None), c)) for c in range(DC)])
                    ins.then_inc(up_ps, 1)
                if not last:
                    transpose_x(e + 1)
                pe.wait_ge(y_done, e)
                for t in range(ST):
                    for f in range(FC):
                        if t == 0:
                            pe.wait_ge(h_lo, FC * e + f + 1)
                        ins = product3(nc, B[6 + t // 2][:, (t % 2) * D:(t % 2 + 1) * D], hT, w3[u],
                                       [((slice(None), f, slice(t * P, (t + 1) * P)), (slice(None), f))], f == 0, f == FC - 1)
                    if t % 2 or t == ST - 1:
                        ins.then_inc(y_ps, 1)

            transpose_x(0)
            turns(pe, turn)

        @block.scalar
        def _(act):
            def high_w(e, u):
                act.wait_ge(w_in, 3 * 16 * (e + 1))
                for src, w in zip(raw, (w1, w2, w3)):
                    nc.scalar.activation(w[u][0][:], src[:], ACT.Copy).then_inc(w_hi, 1)

            def high_x(e):
                act.wait_ge(xT_ps, e + 1)
                act.wait_ge(up_ps, FC * e)
                for c in range(DC):
                    nc.scalar.activation(xT[0][:, c, :], B[c][:, 0:S], ACT.Copy).then_inc(x_hi, 1)

            def high_h(e, f):
                act.wait_ge(h_done, FC * e + f + 1)
                if f == 0:
                    act.wait_ge(y_ps, YP * e)
                nc.scalar.activation(hT[0][:, f, :], h[:, f % 2, :], ACT.Copy).then_inc(h_hi, 1)

            def turn(e, j, u, last):
                for f in range(FC):
                    act.wait_ge(up_ps, FC * e + f + 1)
                    nc.scalar.activation(sg[:, f % 2, :], B[2 + 2 * (f % 2)][:, 0:S], ACT.Silu).then_inc(sg_done, 1)
                    if f:
                        high_h(e, f - 1)
                high_h(e, FC - 1)
                if not last:
                    high_x(e + 1)
                    high_w(e + 1, 1 - u)

            high_w(0, 0)
            high_x(0)
            turns(act, turn)

        @block.vector
        def _(dve):
            def low_w(e, u):
                for i, (src, w) in enumerate(zip(raw, (w1, w2, w3))):
                    dve.wait_ge(w_hi, 3 * e + i + 1)
                    nc.vector.tensor_tensor(w[u][1][:], src[:], w[u][0][:].bitcast(F32), ALU.subtract).then_inc(w_lo, 1)

            def low_x(e):
                for c in range(DC):
                    dve.wait_ge(x_hi, DC * e + c + 1)
                    ins = nc.vector.tensor_tensor(xT[1][:, c, :], B[c][:, 0:S], xT[0][:, c, :].bitcast(F32), ALU.subtract)
                ins.then_inc(x_lo, 1)

            def low_h(e, f):
                dve.wait_ge(h_hi, FC * e + f + 1)
                nc.vector.tensor_tensor(hT[1][:, f, :], h[:, f % 2, :], hT[0][:, f, :].bitcast(F32), ALU.subtract).then_inc(h_lo, 1)

            def turn(e, j, u, last):
                for f in range(FC):
                    dve.wait_ge(sg_done, FC * e + f + 1)
                    if f >= 2:
                        dve.wait_ge(h_lo, FC * e + f - 1)
                    nc.vector.tensor_tensor(h[:, f % 2, :], B[3 + 2 * (f % 2)][:, 0:S], sg[:, f % 2, :], ALU.mult).then_inc(h_done, 1)
                    if f:
                        low_h(e, f - 1)
                low_h(e, FC - 1)
                if not last:
                    low_x(e + 1)
                    low_w(e + 1, 1 - u)
                dve.wait_ge(f_out, 16 * ST * e)
                for t in range(ST):
                    if t % 2 == 0:
                        dve.wait_ge(y_ps, YP * e + t // 2 + 1)
                    ins = nc.vector.tensor_scalar(y[:, t, :], B[6 + t // 2][:, (t % 2) * D:(t % 2 + 1) * D],
                                                  col(k.slot_share, e)[:, t:t + 1], None, ALU.mult)
                ins.then_inc(y_done, 1)

            low_w(0, 0)
            low_x(0)
            turns(dve, turn)


def layer1_prepare(nc, R, k, x_b, s0_b, f0_b, xn_b, v_b, fs_b, qk_d, w):
    sb, sem = R.sb, R.sem
    wq, wk, wv, wr = sb("wq", [P, DC, D]), sb("wk", [P, DC, D]), sb("wv", [P, DC, D]), sb("wr", [P, DC, E1])
    ws1, ws3, ws2 = sb("ws1", [P, DC, FF]), sb("ws3", [P, DC, FF]), sb("ws2", [P, FC, D])
    lnw, lnb, lnw_row, lnb_row = sb("lnw", [P, DC]), sb("lnb", [P, DC]), sb("lnw_row", [P, D]), sb("lnb_row", [P, D])
    x, s0, f0, g = sb("x", [P, T, D]), sb("s0", [P, T, D]), sb("f0", [P, T, D]), sb("g", [P, T, D])
    stats, mv, veps, rstd = sb("stats", [P, T, 6]), sb("mv", [P, T, 2]), sb("veps", [P, T]), sb("rstd", [P, T])
    half, small, ra = sb("half", [P, T]), sb("small", [P, 3, T]), sb("ra", [P, T])
    xn, xa, xas = sb("xn", [P, T, D]), sb("xa", [P, T, D]), sb("xas", [P, T, D])
    xnT, xaT = sb("xnT", [P, DC, S]), sb("xaT", [P, DC, S])
    hi, lo = sb("hi", [P, 2, S], F32R), sb("lo", [P, 2, S], F32R)
    v = sb("v", [P, T, NH, 2 * HD])
    sg, hT = sb("sg", [P, 2, S]), sb("hT", [P, FC, S])
    B = R.banks(8)
    fs = sb("fs", [P, T, D])
    w_in, x_in, xn_out, v_out, fs_out = sem("w_in"), sem("x_in"), sem("xn_out"), sem("v_out"), sem("fs_out")
    part_out = [sem("part_out0"), sem("part_out1")]
    (g_done, sg0_done, x1_done, veps_done, rstd_done, ra_done, xn_done, xa_done, xas_done, xall_done, tr_ps, tr_sb, lg_ps, lg_sb, v_set, v_ps, v_sb,
     qk_ps, hi_done, lo_done, up_ps, sg_done, h_done, y_ps, y_sb, dve1, pool1, half_set) = [
        sem(n) for n in ("g_done", "sg0_done", "x1_done", "veps_done", "rstd_done", "ra_done", "xn_done", "xa_done", "xas_done", "xall_done", "tr_ps", "tr_sb",
                         "lg_ps", "lg_sb", "v_set", "v_ps", "v_sb", "qk_ps", "hi_done", "lo_done", "up_ps", "sg_done", "h_done", "y_ps",
                         "y_sb", "dve1", "pool1", "half_set")]

    def turns(eng, turn):
        turn(0, None)
        with eng.Fori(0, NB - 1) as b:
            turn(b + 1, b)
        turn(None, NB - 1)

    def flat(ap):
        return ap.rearrange("p t d -> p (t d)")

    with nc.Block() as block:

        @block.sync
        def _(sp):
            loads = [(wq, w["wq"]), (wk, w["wk"]), (wv, w["wv"]), (wr, w["Wr"]), (ws1, w["Ws1"]), (ws3, w["Ws3"]), (ws2, w["Ws2"]),
                     (lnw, w["lnw"]), (lnb, w["lnb"]), (lnw_row, w["lnw_row"]), (lnb_row, w["lnb_row"])]

            def load_x(n):
                for buf, src in ((x, x_b), (s0, s0_b), (f0, f0_b)):
                    sp.dma_start(buf[:], at(src, n)).then_inc(x_in, 16)

            LAST = NB - 1
            load_x(0)
            with nc.allow_non_contiguous_dma(reason="two columns of layer norm weights"):
                for buf, src in loads:
                    sp.dma_start(buf[:], src).then_inc(w_in, 16)

            def turn(n, c):
                if c is not None:
                    for i in range(2 * DC):
                        u = i % 2
                        sp.wait_ge(hi_done, 2 * DC * c + i + 1)
                        sp.dma_start(at(qk_d[i], c), hi[:, u, :].bitcast(F32)).then_inc(part_out[u], 16)
                        sp.wait_ge(lo_done, 2 * DC * c + i + 1)
                        sp.dma_start(at(qk_d[2 * DC + i], c), lo[:, u, :].bitcast(F32)).then_inc(part_out[u], 16)
                    sp.wait_ge(v_sb, T * (c + 1))
                    sp.dma_start(at(v_b, c), v[:].rearrange("p t h d -> p t (h d)")).then_inc(v_out, 16)
                if n is not None:
                    sp.wait_ge(xn_done, n + 1)
                    sp.dma_start(at(xn_b, n), xn[:]).then_inc(xn_out, 16)
                    if not (isinstance(n, int) and n == LAST):
                        load_x(n + 1)
                if c is not None:
                    sp.wait_ge(y_sb, 2 * (c + 1))
                    sp.dma_start(at(fs_b, c), fs[:]).then_inc(fs_out, 16)

            turn(0, None)
            with sp.Fori(0, NB - 2) as b:
                turn(b + 1, b)
            turn(LAST, LAST - 1)
            turn(None, NB - 1)
            sp.wait_ge(xn_out, 16 * NB)
            sp.wait_ge(v_out, 16 * NB)
            sp.wait_ge(fs_out, 16 * NB)
            for u in range(2):
                sp.wait_ge(part_out[u], 4 * 16 * NB)

        @block.tensor
        def _(pe):
            def transposed(src, waits, count):
                pe.wait_ge(*waits)
                pe.wait_ge(tr_sb, count)
                for ch in range(DC):
                    for t in range(T):
                        ins = nc.tensor.transpose(B[ch][:, t * P:(t + 1) * P], src[:, t, ch * P:(ch + 1) * P], k.ident[:])
                ins.then_inc(tr_ps, 1)

            def turn(n, c):
                if c is not None:
                    pe.wait_ge(w_in, 11 * 16)
                    pe.wait_ge(tr_sb, 2 * (c + 1))
                    pe.wait_ge(y_sb, 2 * c)
                    for t in range(T):
                        for ch in range(DC):
                            ins = nc.tensor.matmul(B[6][:, t * E1:(t + 1) * E1], xnT[:, ch, t * P:(t + 1) * P], wr[:, ch, :],
                                                   start=ch == 0, stop=ch == DC - 1)
                    ins.then_inc(lg_ps, 1)
                    pe.wait_ge(h_done, FC * c)
                    for i in range(2 * DC):
                        for ch in range(DC):
                            ins = nc.tensor.matmul(B[2 + i][:], (wq, wk)[i // DC][:, ch, (i % DC) * P:(i % DC + 1) * P], xaT[:, ch, :],
                                                   start=ch == 0, stop=ch == DC - 1)
                        ins.then_inc(qk_ps, 1)
                    for t in range(T):
                        if t == 1:
                            pe.wait_ge(lg_sb, c + 1)
                        if t >= 2:
                            pe.wait_ge(v_sb, T * c + t - 1)
                        for ch in range(DC):
                            ins = nc.tensor.matmul(B[7 - t % 2][:, 0:D], xaT[:, ch, t * P:(t + 1) * P], wv[:, ch, :],
                                                   start=ch == 0, stop=ch == DC - 1)
                        ins.then_inc(v_ps, 1)
                    for f in range(FC):
                        gate, value = B[2 + 2 * (f % 2)], B[3 + 2 * (f % 2)]
                        if f < 2:
                            pe.wait_ge(lo_done, 2 * DC * c + 2 * f + 2)
                        else:
                            pe.wait_ge(h_done, FC * c + f - 1)
                        for bank, wt in ((gate, ws3), (value, ws1)):
                            for ch in range(DC):
                                ins = nc.tensor.matmul(bank[:], wt[:, ch, f * P:(f + 1) * P], xnT[:, ch, :], start=ch == 0, stop=ch == DC - 1)
                        ins.then_inc(up_ps, 1)
                if n is not None:
                    transposed(xn, (xn_done, n + 1), 2 * n)
                    transposed(xa, (xa_done, n + 1), 2 * n + 1)
                if c is not None:
                    pe.wait_ge(h_done, FC * (c + 1))
                    pe.wait_ge(v_sb, T * (c + 1))
                    for t in range(T):
                        for f in range(FC):
                            ins = nc.tensor.matmul(B[6 + t // 2][:, (t % 2) * D:(t % 2 + 1) * D], hT[:, f, t * P:(t + 1) * P], ws2[:, f, :],
                                                   start=f == 0, stop=f == FC - 1)
                        if t % 2:
                            ins.then_inc(y_ps, 1)

            turns(pe, turn)

        @block.scalar
        def _(act):
            def turn(n, c):
                if c is not None:
                    for i in range(2 * DC):
                        act.wait_ge(qk_ps, 2 * DC * c + i + 1)
                        act.wait_ge(part_out[i % 2], 2 * 16 * (DC * c + i // 2))
                        nc.scalar.activation(hi[:, i % 2, :], B[2 + i][:], ACT.Copy).then_inc(hi_done, 1)
                if n is not None:
                    act.wait_ge(x_in, 3 * 16 * (n + 1))
                    act.wait_ge(sg0_done, n)
                    nc.scalar.activation(g[:], f0[:], ACT.Silu).then_inc(g_done, 1)
                if c is not None:
                    for f in range(FC):
                        act.wait_ge(up_ps, FC * c + f + 1)
                        act.wait_ge(h_done, FC * c + max(f - 1, 0))
                        nc.scalar.activation(sg[:, f % 2, :], B[2 + 2 * (f % 2)][:], ACT.Silu).then_inc(sg_done, 1)
                if n is not None:
                    act.wait_ge(tr_ps, 2 * n + 1)
                    if c is not None:
                        act.wait_ge(up_ps, FC * (c + 1))
                    for ch in range(DC):
                        ins = nc.scalar.activation(xnT[:, ch, :], B[ch][:], ACT.Copy)
                    ins.then_inc(tr_sb, 1)
                    act.wait_ge(w_in, 11 * 16)
                    act.wait_ge(tr_ps, 2 * n + 2)
                    for ch in range(DC):
                        ins = nc.scalar.activation(xaT[:, ch, :], B[ch][:], ACT.Identity, scale=lnw[:, ch:ch + 1], bias=lnb[:, ch:ch + 1])
                    ins.then_inc(tr_sb, 1)

            turns(act, turn)

        @block.gpsimd
        def _(pool):
            nc.gpsimd.memset(v[:, :, :, HD:2 * HD], 0.0).then_inc(v_set, 1)
            nc.gpsimd.memset(half[:], -0.5).then_inc(half_set, 1)
            pool.wait_ge(v_set, 1)
            nc.gpsimd.memset(v[:, :, :, HD:HD + 1], 1.0).then_inc(v_set, 1)
            pool.wait_ge(half_set, 1)

            def turn(n, c):
                if n is None:
                    return
                own = Steps(pool, pool1, 3, n)
                pool.wait_ge(veps_done, n + 1)
                pool.wait_ge(xn_done, n)
                nc.gpsimd.tensor_tensor(rstd[:], veps[:], half[:], ALU.pow).then_inc(rstd_done, 1)
                pool.wait_ge(rstd_done, n + 1)
                own.step(nc.gpsimd.tensor_tensor(small[:, 0, :], rstd[:], rstd[:], ALU.mult))
                own.wait()
                own.step(nc.gpsimd.tensor_tensor(small[:, 1, :], small[:, 0, :], mv[:, :, 1], ALU.mult))
                own.wait()
                land(pool, k)
                own.step(nc.gpsimd.tensor_scalar(small[:, 2, :], small[:, 1, :], LN1_EPS, None, ALU.add))
                own.wait()
                own.end()
                pool.wait_ge(xa_done, n)
                nc.gpsimd.tensor_tensor(ra[:], small[:, 2, :], half[:], ALU.pow).then_inc(ra_done, 1)
                pool.wait_ge(w_in, 11 * 16)
                pool.wait_ge(xa_done, n + 1)
                for t in range(T):
                    ins = nc.gpsimd.tensor_tensor(xas[:, t, :], xa[:, t, :], lnw_row[:], ALU.mult)
                ins.then_inc(xas_done, 1)
                pool.wait_ge(xas_done, n + 1)
                for t in range(T):
                    ins = nc.gpsimd.tensor_tensor(col(k.xa_all, n)[:, t, :], xas[:, t, :], lnb_row[:], ALU.add)
                ins.then_inc(xall_done, 1)

            turns(pool, turn)

        @block.vector
        def _(dve):
            def turn(n, c):
                if c is not None:
                    dve.wait_ge(lg_ps, c + 1)
                    nc.vector.tensor_copy(k.logits1[:, bass.ds(c, 1)].rearrange("p o t e -> p (o t e)"), B[6][:, 0:T * E1]).then_inc(lg_sb, 1)
                    for i in range(2 * DC):
                        dve.wait_ge(hi_done, 2 * DC * c + i + 1)
                        nc.vector.tensor_tensor(lo[:, i % 2, :], B[2 + i][:], hi[:, i % 2, :].bitcast(F32), ALU.subtract).then_inc(lo_done, 1)
                    dve.wait_ge(v_out, 16 * c)
                    for t in range(T):
                        dve.wait_ge(v_ps, T * c + t + 1)
                        nc.vector.tensor_copy(v[:, t, :, 0:HD], B[7 - t % 2][:, 0:D].rearrange("p (h d) -> p h d", d=HD)).then_inc(v_sb, 1)
                if n is not None:
                    own = Steps(dve, dve1, 2 * T, n)
                    x1 = col(k.x1_all, n)
                    dve.wait_ge(g_done, n + 1)
                    nc.vector.tensor_tensor(flat(g[:]), flat(g[:]), flat(s0[:]), ALU.mult).then_inc(sg0_done, 1)
                    dve.wait_ge(sg0_done, n + 1)
                    nc.vector.tensor_tensor(flat(x1), flat(g[:]), flat(x[:]), ALU.add).then_inc(x1_done, 1)
                    dve.wait_ge(x1_done, n + 1)
                    dve.wait_ge(ra_done, n)
                    normalise_stats(nc, own, k, x1, stats, mv)
                    own.wait()
                    own.end()
                    nc.vector.tensor_scalar(veps[:], mv[:, :, 1], LN_EPS, None, ALU.add).then_inc(veps_done, 1)

                def hidden(f):
                    dve.wait_ge(sg_done, FC * c + f + 1)
                    if f == 0:
                        dve.wait_ge(y_ps, 2 * c)
                    nc.vector.tensor_tensor(hT[:, f, :], B[3 + 2 * (f % 2)][:], sg[:, f % 2, :], ALU.mult).then_inc(h_done, 1)

                if c is not None:
                    hidden(0)
                    hidden(1)
                if n is not None:
                    dve.wait_ge(rstd_done, n + 1)
                    dve.wait_ge(xn_out, 16 * n)
                    dve.wait_ge(tr_ps, 2 * n)
                    for t in range(T):
                        ins = nc.vector.tensor_scalar(xn[:, t, :], x1[:, t, :], mv[:, t, 0:1], rstd[:, t:t + 1], ALU.subtract, ALU.mult)
                    ins.then_inc(xn_done, 1)
                    dve.wait_ge(xn_done, n + 1)
                    dve.wait_ge(ra_done, n + 1)
                    dve.wait_ge(xas_done, n)
                    for t in range(T):
                        ins = nc.vector.tensor_scalar(xa[:, t, :], xn[:, t, :], ra[:, t:t + 1], None, ALU.mult)
                    ins.then_inc(xa_done, 1)
                if c is not None:
                    hidden(2)
                    hidden(3)
                    for i in range(2):
                        dve.wait_ge(y_ps, 2 * c + i + 1)
                        if i == 0:
                            dve.wait_ge(fs_out, 16 * c)
                        nc.vector.tensor_copy(flat(fs[:, 2 * i:2 * i + 2, :]), B[6 + i][:]).then_inc(y_sb, 1)

            dve.wait_ge(v_set, 2)
            turns(dve, turn)


def layer1_attention(nc, R, k, qk_v, v_v, o_v, xn_b, xs_rows):
    sb, sem = R.sb, R.sem
    R4, M0 = 4 * HD, 96
    KR = M0 + 2
    qa = [sb(f"qa{i}", [P, QH, S], F32R) for i in range(NQ)]
    ka = [sb(f"ka{i}", [P, QH, S], F32R) for i in range(NQ)]
    va = [sb(f"va{i}", [P, T, QH * 2 * HD]) for i in range(NQ)]
    prob = [sb(f"prob{i}", [P, QH, 2, S]) for i in range(2)]
    neg_max = sb("neg_max", [P, 2, QH * T])
    mh, ml = sb("mh", [QH * T, P], F32R), sb("ml", [QH * T, P], F32R)
    oT, den, o = sb("oT", [P, S]), sb("den", [P, T * QH]), sb("o", [P, T, QH, HD])
    rows, slots = sb("rows", [P, T, ROW]), sb("slots", [P, TOP, T], U32)
    rows_in, rows_out, slots_set, weight_set = sem("rows_in"), sem("rows_out"), sem("slots_set"), sem("weight_set")
    B = R.banks(8)
    q_in = [sem(f"q_in{i}") for i in range(NQ)]
    m_in = [sem(f"m_in{i}") for i in range(NQ)]
    q_set, k_set, p1_ps, mx_done, mT_ps, mh_done, ml_done, s_ps, p_done, pv_ps, oT_sb, oT_ps, den_done, o_done, o_out = [
        sem(n) for n in ("q_set", "k_set", "p1_ps", "mx_done", "mT_ps", "mh_done", "ml_done", "s_ps", "p_done", "pv_ps", "oT_sb", "oT_ps",
                         "den_done", "o_done", "o_out")]
    NU = 8

    def batches(eng, first, turn, last):
        first()
        for q in range(NQ):
            turn(0, q, True)
        with eng.Fori(1, NB - 1) as b:
            for q in range(NQ):
                turn(b, q, True)
        for q in range(NQ):
            turn(NB - 1, q, False)
        last()

    def before(b, q):
        if q:
            return b, q - 1
        return None if isinstance(b, int) and b == 0 else (b - 1, NQ - 1)

    def ahead(b, q, d, more):
        if q + d < NQ:
            return b, q + d
        return (b + 1, q + d - NQ) if more else None

    with nc.Block() as block:

        @block.sync
        def _(sp):
            def load(b, q):
                for r in range(4):
                    sp.dma_start(qa[q][r * HD:(r + 1) * HD].bitcast(F32), at(qk_v[r // 2][0][q], b)).then_inc(q_in[q], 16)
                    sp.dma_start(ka[q][r * HD:(r + 1) * HD].bitcast(F32), at(qk_v[r % 2][1][q], b)).then_inc(q_in[q], 16)
                sp.dma_start(va[q][:], at(v_v[q], b)).then_inc(q_in[q], 16)

            def max_rows(b, q):
                g = b * NQ + q
                sp.wait_ge(mh_done, g + 1)
                sp.dma_start(qa[q][M0:M0 + 1].bitcast(F32), mh[:].bitcast(F32)).then_inc(m_in[q], 16)
                sp.wait_ge(ml_done, g + 1)
                sp.dma_start(qa[q][M0 + 1:M0 + 2].bitcast(F32), ml[:].bitcast(F32)).then_inc(m_in[q], 16)

            def first():
                for q in range(NQ):
                    load(0, q)
                max_rows(0, 0)

            def store(b, q):
                sp.wait_ge(o_done, b * NQ + q + 1)
                with nc.allow_non_contiguous_dma(reason="four heads of each row"):
                    sp.dma_start(at(o_v[q], b), o[:].rearrange("p t h d -> p t (h d)")).then_inc(o_out, 16)

            def turn(b, q, more):
                one, prev = ahead(b, q, 1, more), before(b, q)
                if prev and (more or q == 0):
                    sp.wait_ge(pv_ps, 2 * (prev[0] * NQ + prev[1] + 1))
                    load(prev[0] + 1, prev[1])
                if one:
                    max_rows(*one)
                if prev:
                    store(*prev)

            batches(sp, first, turn, lambda: store(NB - 1, NQ - 1))
            sp.wait_ge(o_out, 16 * NB * NQ)

        @block.gpsimd
        def _(pool):
            for i in range(NQ):
                ins = nc.gpsimd.memset(qa[i][R4:M0].bitcast(F32), 0.0)
            ins.then_inc(q_set, 1)
            pool.wait_ge(q_set, 1)

            with pool.Fori(0, NB) as b:
                pool.dma_start(rows[:, :, 0:D], at(xn_b, b)).then_inc(rows_in, 16)
                nc.gpsimd.tensor_copy(slots[:], col(k.slot1, b)).then_inc(slots_set, 1)
                nc.gpsimd.tensor_copy(rows[:].bitcast(I32)[:, :, D], k.token[:].rearrange("p (b t) -> p b t", t=T)[:, bass.ds(b, 1)].rearrange("p o t -> p (o t)")).then_inc(slots_set, 1)
                for i in range(TOP):
                    nc.gpsimd.tensor_copy(rows[:, :, D + 1], k.weight[:, i, :].rearrange("p (b t) -> p b t", t=T)[:, bass.ds(b, 1)].rearrange("p o t -> p (o t)")).then_inc(weight_set, 1)
                    pool.wait_ge(weight_set, TOP * b + i + 1)
                    if i == 0:
                        pool.wait_ge(slots_set, 2 * (b + 1))
                        pool.wait_ge(rows_in, 16 * (b + 1))
                    land(pool, k)
                    for t in range(T):
                        nc.gpsimd.indirect_dma_start(xs_rows, bass.IndirectOffsetOnAxis(slots[:, i, t:t + 1], 0), rows[:, t, :], None).then_inc(rows_out, 16)
                    pool.wait_ge(rows_out, (TOP * b + i + 1) * T * 16)
                    land(pool, k)

        @block.tensor
        def _(pe):
            def scores1(g, q, h, t, wait):
                s = g * QH * T + h * T + t
                if wait:
                    pe.wait_ge(mx_done, s - 1)
                nc.tensor.matmul(B[t % 2][:], qa[q][0:M0, h, t * P:(t + 1) * P], ka[q][0:M0, h, :], start=True, stop=True).then_inc(p1_ps, 1)

            def half1(b, q, second, i):
                g = b * NQ + q
                if not second and i == 0:
                    pe.wait_ge(q_in[q], 9 * 16 * (b + 1))
                h = (2 if second else 0) + i // 2
                for t in (2 * (i % 2), 2 * (i % 2) + 1):
                    scores1(g, q, h, t, not (isinstance(g, int) and g == 0 and h == 0 and t < 2))

            def transpose_max(b, q):
                g = b * NQ + q
                pe.wait_ge(mx_done, QH * T * (g + 1))
                if not (isinstance(g, int) and g < 2):
                    pe.wait_ge(o_done, g - 2)
                nc.tensor.transpose(B[7][0:QH * T, 0:P], neg_max[:, q % 2, :], k.ident[:]).then_inc(mT_ps, 1)

            def weigh(b, q, jp):
                g = b * NQ + q
                if jp == 0:
                    pe.wait_ge(oT_sb, g)
                pe.wait_ge(p_done, NU * g + 4 * (jp + 1))
                for jj in range(2):
                    j = 2 * jp + jj
                    for h in range(QH):
                        rows = slice(32 * h, 32 * h + 32)
                        ins = nc.tensor.matmul(B[6][rows, :], va[q][:, j, rows], prob[jp][:, h, jj, :], start=j == 0, stop=j == T - 1,
                                               tile_position=(0, 32 * h))
                ins.then_inc(pv_ps, 1)

            def transpose_o(b, q, one):
                g = b * NQ + q
                pe.wait_ge(oT_sb, g + 1)
                if one:
                    pe.wait_ge(ml_done, g + 3)
                else:
                    pe.wait_ge(o_done, g)
                for t in range(T):
                    ins = nc.tensor.transpose(B[7][:, t * P:(t + 1) * P], oT[:, t * P:(t + 1) * P], k.ident[:])
                ins.then_inc(oT_ps, 1)

            def first():
                pe.wait_ge(q_set, 1)
                pe.wait_ge(k_set, 1)
                for i in range(4):
                    half1(0, 0, False, i)
                for i in range(4):
                    half1(0, 0, True, i)
                transpose_max(0, 0)
                for i in range(4):
                    half1(0, 1, False, i)

            def turn(b, q, more):
                g = b * NQ + q
                one, two, prev = ahead(b, q, 1, more), ahead(b, q, 2, more), before(b, q)
                pe.wait_ge(m_in[q], 2 * 16 * (b + 1))
                for u in range(NU):
                    jp, h = u // QH, u % QH
                    if prev or u > 1:
                        pe.wait_ge(p_done, NU * g + u - 1)
                    for jj in range(2):
                        j = 2 * jp + jj
                        ins = nc.tensor.matmul(B[2 + 2 * (u % 2) + jj][:], ka[q][0:KR, h, j * P:(j + 1) * P], qa[q][0:KR, h, :], start=True, stop=True)
                    ins.then_inc(s_ps, 1)
                    if u < 4 and one:
                        half1(*one, True, u)
                    if u >= 4 and two:
                        half1(*two, False, u - 4)
                    if u == 1 and prev:
                        weigh(*prev, 1)
                    if u == 4 and one:
                        transpose_max(*one)
                    if u == 5:
                        weigh(b, q, 0)
                        if prev:
                            transpose_o(*prev, one)

            def last():
                weigh(NB - 1, NQ - 1, 1)
                transpose_o(NB - 1, NQ - 1, None)

            batches(pe, first, turn, last)

        @block.scalar
        def _(act):
            def copy_o(b, q):
                g = b * NQ + q
                act.wait_ge(pv_ps, 2 * (g + 1))
                act.wait_ge(oT_ps, g)
                nc.scalar.activation(oT[:], B[6][:], ACT.Copy).then_inc(oT_sb, 1)

            def turn(b, q, more):
                g = b * NQ + q
                prev = before(b, q)
                for u in range(NU):
                    jp, h = u // QH, u % QH
                    act.wait_ge(s_ps, NU * g + u + 1)
                    if h == 0 and prev:
                        act.wait_ge(pv_ps, 2 * g + jp - 1)
                    for jj in range(2):
                        ins = nc.scalar.activation(prob[jp][:, h, jj, :], B[2 + 2 * (u % 2) + jj][:], ACT.Exp, scale=float(D) ** -0.5)
                    ins.then_inc(p_done, 1)
                    if u == 3 and prev:
                        copy_o(*prev)

            batches(act, lambda: None, turn, lambda: copy_o(NB - 1, NQ - 1))

        @block.vector
        def _(dve):
            for i in range(NQ):
                nc.vector.memset(ka[i][R4:M0].bitcast(F32), 0.0)
                ins = nc.vector.memset(ka[i][M0:KR].bitcast(F32), 1.0)
            ins.then_inc(k_set, 1)

            def maxima(b, q, second, i):
                g = b * NQ + q
                h = (2 if second else 0) + i // 2
                for t in (2 * (i % 2), 2 * (i % 2) + 1):
                    s = g * QH * T + h * T + t
                    dve.wait_ge(p1_ps, s + 1)
                    nc.vector.tensor_reduce(neg_max[:, q % 2, h * T + t:h * T + t + 1], B[t % 2][:], AX.X, ALU.max, negate=True).then_inc(mx_done, 1)

            def split_max(b, q):
                g = b * NQ + q
                dve.wait_ge(mT_ps, g + 1)
                if not (isinstance(g, int) and g == 0):
                    pb = (b, q - 1) if q else (b - 1, NQ - 1)
                    dve.wait_ge(m_in[pb[1]], 2 * 16 * (pb[0] + 1))
                nc.vector.tensor_copy(mh[:], B[7][0:QH * T, 0:P]).then_inc(mh_done, 1)
                dve.wait_ge(mh_done, g + 1)
                nc.vector.tensor_tensor(ml[:], B[7][0:QH * T, 0:P], mh[:].bitcast(F32), ALU.subtract).then_inc(ml_done, 1)

            def first():
                for i in range(4):
                    maxima(0, 0, False, i)
                for i in range(4):
                    maxima(0, 0, True, i)
                split_max(0, 0)
                for i in range(4):
                    maxima(0, 1, False, i)

            def divide(b, q):
                g = b * NQ + q
                dve.wait_ge(oT_ps, g + 1)
                v = B[7][:].rearrange("p (t h d) -> p (t h) d", t=T, h=QH)
                nc.vector.reciprocal(den[:], v[:, :, HD]).then_inc(den_done, 1)
                dve.wait_ge(den_done, g + 1)
                dve.wait_ge(o_out, 16 * g)
                nc.vector.tensor_tensor(o[:].rearrange("p t h d -> p (t h) d"), v[:, :, 0:HD],
                                        den[:].unsqueeze(2).broadcast_to([P, T * QH, HD]), ALU.mult).then_inc(o_done, 1)

            def turn(b, q, more):
                one, two, prev = ahead(b, q, 1, more), ahead(b, q, 2, more), before(b, q)
                if one:
                    for i in range(4):
                        maxima(*one, True, i)
                if two:
                    maxima(*two, False, 0)
                if one:
                    split_max(*one)
                if two:
                    maxima(*two, False, 1)
                if prev:
                    divide(*prev)
                if two:
                    maxima(*two, False, 2)
                    maxima(*two, False, 3)

            batches(dve, first, turn, lambda: divide(NB - 1, NQ - 1))


def layer1_route(nc, R, k, rb_row):
    sb, sem = R.sb, R.sem
    assert TOP == 2
    row, scaled, biased = sb("row", [P, E1]), sb("scaled", [P, NT, E1]), sb("biased", [P, NT, E1])
    best, place = sb("best", [P, NT, 8]), sb("place", [P, NT, 8], U32)
    number, numberf = sb("number", [P, E1], I32), sb("numberf", [P, E1])
    group, groupf = sb("group", [P, NG], I32), sb("groupf", [P, NG])
    chosen = sb("chosen", [P, NT, TOP])
    hot = [sb(f"hot{i}", [P, NT, E1]) for i in range(TOP)]
    tmp, both, strict = sb("tmp", [P, NT, E1]), sb("both", [P, NT, E1]), sb("strict", [P, P])
    lg, ex, top, total = sb("lg", [P, TOP, NT]), sb("ex", [P, TOP, NT]), sb("top", [P, NT]), sb("total", [P, NT])
    run = [sb(f"run{i}", [P, NT, E1]) for i in range(2)]
    tile_total = sb("tile_total", [P, NT, E1])
    cnt, cnti, ng, ones8, upto, base = sb("cnt", [P, E1]), sb("cnti", [P, E1], I32), sb("ng", [P, E1]), sb("ones8", [P, E1]), sb("upto", [P, E1]), sb("base", [P, E1])
    past, owner, ownerf, slot = sb("past", [P, NG, E1]), sb("owner", [P, NG]), sb("ownerf", [P, NG]), sb("slot", [P, NT])
    B = R.banks(2)
    made, rb_in, exp_in, exp_done, counted, ranks, own_sem = [sem(n) for n in ("made", "rb_in", "exp_in", "exp_done", "counted", "ranks", "dve")]

    def over(ap, shape, axis):
        return ap.unsqueeze(axis).broadcast_to(shape)

    with nc.Block() as block:

        @block.sync
        def _(sp):
            sp.dma_start(row[:], rb_row).then_inc(rb_in, 16)

        @block.gpsimd
        def _(pool):
            nc.gpsimd.iota(number[:], pattern=[[1, E1]], base=0, channel_multiplier=0).then_inc(made, 1)
            nc.gpsimd.iota(group[:], pattern=[[1, NG]], base=0, channel_multiplier=0).then_inc(made, 1)
            nc.gpsimd.tensor_tensor(strict[:], k.upper[:], k.ident[:], ALU.subtract).then_inc(made, 1)

        @block.tensor
        def _(pe):
            pe.wait_ge(counted, 1)
            flat = both[:].rearrange("p n e -> p (n e)")
            nc.tensor.matmul(B[0][:, 0:NT * E1], strict[:], flat, start=True, stop=True)
            nc.tensor.matmul(B[1][:, 0:NT * E1], k.ones[:], flat, start=True, stop=True).then_inc(ranks, 1)

        @block.scalar
        def _(act):
            act.wait_ge(exp_in, 1)
            nc.scalar.activation(ex[:], lg[:], ACT.Exp).then_inc(exp_done, 1)

        @block.vector
        def _(dve):
            own = Steps(dve, own_sem, 0, 0)

            def do(ins):
                own.step(ins)
                own.wait()

            v = nc.vector
            dve.wait_ge(made, 3)
            dve.wait_ge(rb_in, 16)
            own.step(v.tensor_copy(numberf[:], number[:]))
            own.step(v.tensor_copy(groupf[:], group[:]))
            own.step(v.memset(ones8[:], 1.0))
            do(v.tensor_scalar(scaled[:], k.logits1[:].rearrange("p b t e -> p (b t) e"), float(D) ** -0.5, None, ALU.mult))
            do(v.tensor_tensor(biased[:], scaled[:], over(row[:], [P, NT, E1], 1), ALU.add))
            for n in range(NT):
                own.step(v.max(best[:, n, :], biased[:, n, :]))
            for n in range(NT):
                own.wait(NT - 1)
                own.step(v.max_index(place[:, n, :], best[:, n, :], biased[:, n, :]))
            own.wait()
            do(v.tensor_copy(chosen[:], place[:, :, 0:TOP]))
            for i in range(TOP):
                own.step(v.tensor_tensor(hot[i][:], over(numberf[:], [P, NT, E1], 1), over(chosen[:, :, i], [P, NT, E1], 2), ALU.is_equal))
            own.wait()
            v.tensor_tensor(both[:], hot[0][:], hot[1][:], ALU.add).then_inc(counted, 1)
            for i in range(TOP):
                do(v.tensor_tensor(tmp[:], hot[i][:], scaled[:], ALU.mult))
                do(v.tensor_reduce(lg[:, i, :], tmp[:], AX.X, ALU.add))
            do(v.tensor_tensor(top[:], lg[:, 0, :], lg[:, 1, :], ALU.max))
            for i in range(TOP):
                ins = v.tensor_tensor(lg[:, i, :], lg[:, i, :], top[:], ALU.subtract)
            ins.then_inc(exp_in, 1)
            dve.wait_ge(exp_done, 1)
            do(v.tensor_tensor(total[:], ex[:, 0, :], ex[:, 1, :], ALU.add))
            do(v.reciprocal(top[:], total[:]))
            for i in range(TOP):
                own.step(v.tensor_tensor(k.weight[:, i, :], ex[:, i, :], top[:], ALU.mult))
            dve.wait_ge(ranks, 1)
            do(v.tensor_copy(tile_total[:].rearrange("p n e -> p (n e)"), B[1][:, 0:NT * E1]))
            src, step, turn = tile_total, 1, 0
            while step < NT:
                dst = run[turn % 2]
                own.step(v.tensor_copy(dst[:, 0:step, :], src[:, 0:step, :]))
                do(v.tensor_tensor(dst[:, step:, :], src[:, step:, :], src[:, 0:NT - step, :], ALU.add))
                src, step, turn = dst, 2 * step, turn + 1
            do(v.tensor_scalar(cnt[:], src[:, NT - 1, :], float(GS - 1), None, ALU.add))
            do(v.tensor_copy(cnti[:], cnt[:]))
            do(v.tensor_scalar(cnti[:], cnti[:], GS.bit_length() - 1, None, ALU.arith_shift_right))
            do(v.tensor_copy(ng[:], cnti[:]))
            do(v.tensor_tensor_scan(upto[:], ones8[:], ng[:], 0.0, ALU.mult, ALU.add))
            do(v.tensor_tensor(base[:], upto[:], ng[:], ALU.subtract))
            do(v.tensor_tensor(past[:], over(upto[:], [P, NG, E1], 1), over(groupf[:], [P, NG, E1], 2), ALU.is_le))
            do(v.tensor_reduce(owner[:], past[:], AX.X, ALU.add))
            do(v.tensor_scalar(ownerf[:], owner[:], float(E1 - 1), None, ALU.min))
            own.step(v.tensor_copy(k.owner[:], ownerf[:]))
            do(v.tensor_scalar(base[:], base[:], float(GS), None, ALU.mult))
            do(v.tensor_tensor(tmp[:], src[:], tile_total[:], ALU.subtract))
            do(v.tensor_tensor(tmp[:].rearrange("p n e -> p (n e)"), B[0][:, 0:NT * E1], tmp[:].rearrange("p n e -> p (n e)"), ALU.add))
            do(v.tensor_tensor(tmp[:], tmp[:], over(base[:], [P, NT, E1], 1), ALU.add))
            for i in range(TOP):
                do(v.tensor_tensor(hot[i][:], hot[i][:], tmp[:], ALU.mult))
                do(v.tensor_reduce(slot[:], hot[i][:], AX.X, ALU.add))
                do(v.tensor_copy(k.slot1[:, :, i, :], slot[:].rearrange("p (b t) -> p b t", t=T)))


def layer1_experts(nc, R, k, xs_g, f_rows, w1_d, w2_d, w3_d):
    sb, sem = R.sb, R.sem
    GT = GS // P
    YP = (GT + 1) // 2
    raw = [sb(f"raw{i}", s) for i, s in enumerate(([P, DC, FF], [P, DC, FF], [P, FC, D]))]
    w1, w3, w2 = [[[sb(f"{n}{u}{part}", s, F32R) for part in ("hi", "lo")] for u in range(2)] for n, s in (("w1", [P, DC, FF]), ("w3", [P, DC, FF]), ("w2", [P, FC, D]))]
    xT, hT = [[sb(n + part, s, F32R) for part in ("hi", "lo")] for n, s in (("xT", [P, DC, GS]), ("hT", [P, FC, GS]))]
    h = sb("h", [P, 2, GS])
    xg, sg, y = sb("xg", [P, GT, ROW]), sb("sg", [P, 2, GS]), sb("y", [P, GT, D])
    B = R.banks(8)
    w_in = sem("w_in")
    token, weight = [sb(f"token{u}", [P, GT], U32) for u in range(2)], [sb(f"weight{u}", [P, GT]) for u in range(2)]
    xg_in, f_out, marks_set = sem("xg_in"), sem("f_out"), sem("marks_set")
    xT_ps, x_hi, x_lo, w_hi, w_lo, up_ps, sg_done, h_done, h_hi, h_lo, y_ps, y_done = [
        sem(n) for n in ("xT_ps", "x_hi", "x_lo", "w_hi", "w_lo", "up_ps", "sg_done", "h_done", "h_hi", "h_lo", "y_ps", "y_done")]
    PAIRS = (NG - 2) // 2

    def turns(eng, turn):
        with eng.Fori(0, PAIRS) as j:
            for u in range(2):
                turn(2 * j + u, j, u)
        for g in range(2 * PAIRS, NG):
            turn(g, g // 2, g % 2)

    def is_last(g, n=1):
        return isinstance(g, int) and g + n >= NG

    with nc.Block() as block:

        @block.sync
        def _(sp):
            def load_weights(g):
                e = sp.value_load(k.owner[0:1, bass.ds(g, 1)], min_val=0, max_val=E1 - 1)
                for buf, src in zip(raw, (w3_d, w1_d, w2_d)):
                    sp.dma_start(buf[:], at(src, e)).then_inc(w_in, 16)

            sp.dma_start(xg[:], at(xs_g, 0)).then_inc(xg_in, 16)
            load_weights(0)

            def turn(g, j, u):
                if not is_last(g):
                    sp.wait_ge(xT_ps, g + 1)
                    sp.wait_ge(marks_set, g + 1)
                    sp.dma_start(xg[:], at(xs_g, g + 1)).then_inc(xg_in, 16)
                    sp.wait_ge(w_lo, 3 * (g + 1))
                    load_weights(g + 1)

            turns(sp, turn)

        @block.gpsimd
        def _(pool):
            def marks(g, u):
                pool.wait_ge(xg_in, 16 * (g + 1))
                land(pool, k)
                nc.gpsimd.tensor_copy(token[u][:], xg[:].bitcast(U32)[:, :, D])
                nc.gpsimd.tensor_copy(weight[u][:], xg[:, :, D + 1]).then_inc(marks_set, 1)

            def turn(g, j, u):
                pool.wait_ge(f_out, 16 * GT * g)
                if not is_last(g):
                    marks(g + 1, 1 - u)
                pool.wait_ge(marks_set, g + 1)
                pool.wait_ge(y_done, g + 1)
                land(pool, k)
                for t in range(GT):
                    nc.gpsimd.indirect_dma_start(f_rows, bass.IndirectOffsetOnAxis(token[u][:, t:t + 1], 0), y[:, t, :], None,
                                                 compute_op=ALU.add).then_inc(f_out, 16)

            marks(0, 0)
            turns(pool, turn)
            pool.wait_ge(f_out, 16 * GT * NG)

        @block.tensor
        def _(pe):
            def transpose_x(g):
                pe.wait_ge(xg_in, 16 * (g + 1))
                pe.wait_ge(x_lo, g)
                for c in range(DC):
                    for t in range(GT):
                        ins = nc.tensor.transpose(B[c][:, t * P:(t + 1) * P], xg[:, t, c * P:(c + 1) * P], k.ident[:])
                ins.then_inc(xT_ps, 1)

            def turn(g, j, u):
                pe.wait_ge(w_lo, 3 * (g + 1))
                pe.wait_ge(x_lo, g + 1)
                for f in range(FC):
                    gate, value = B[2 + 2 * (f % 2)], B[3 + 2 * (f % 2)]
                    pe.wait_ge(h_done, FC * g + max(f - 1, 0))
                    for bank, w in ((gate, w3), (value, w1)):
                        ins = product3(nc, bank[:, 0:GS], w[u], xT, [((slice(None), c, slice(f * P, (f + 1) * P)), (slice(None), c)) for c in range(DC)])
                    ins.then_inc(up_ps, 1)
                if not is_last(g):
                    transpose_x(g + 1)
                pe.wait_ge(y_done, g)
                for t in range(GT):
                    for f in range(FC):
                        if t == 0:
                            pe.wait_ge(h_lo, FC * g + f + 1)
                        ins = product3(nc, B[6 + t // 2][:, (t % 2) * D:(t % 2 + 1) * D], hT, w2[u],
                                       [((slice(None), f, slice(t * P, (t + 1) * P)), (slice(None), f))], f == 0, f == FC - 1)
                    if t % 2 or t == GT - 1:
                        ins.then_inc(y_ps, 1)

            transpose_x(0)
            turns(pe, turn)

        @block.scalar
        def _(act):
            def high_w(g, u):
                act.wait_ge(w_in, 3 * 16 * (g + 1))
                for src, w in zip(raw, (w3, w1, w2)):
                    nc.scalar.activation(w[u][0][:], src[:], ACT.Copy).then_inc(w_hi, 1)

            def high_x(g):
                act.wait_ge(xT_ps, g + 1)
                act.wait_ge(up_ps, FC * g)
                for c in range(DC):
                    nc.scalar.activation(xT[0][:, c, :], B[c][:, 0:GS], ACT.Copy).then_inc(x_hi, 1)

            def high_h(g, f):
                act.wait_ge(h_done, FC * g + f + 1)
                if f == 0:
                    act.wait_ge(y_ps, YP * g)
                nc.scalar.activation(hT[0][:, f, :], h[:, f % 2, :], ACT.Copy).then_inc(h_hi, 1)

            def turn(g, j, u):
                for f in range(FC):
                    act.wait_ge(up_ps, FC * g + f + 1)
                    nc.scalar.activation(sg[:, f % 2, :], B[2 + 2 * (f % 2)][:, 0:GS], ACT.Silu).then_inc(sg_done, 1)
                    if f:
                        high_h(g, f - 1)
                high_h(g, FC - 1)
                if not is_last(g):
                    high_x(g + 1)
                    high_w(g + 1, 1 - u)

            high_w(0, 0)
            high_x(0)
            turns(act, turn)

        @block.vector
        def _(dve):
            def low_w(g, u):
                for i, (src, w) in enumerate(zip(raw, (w3, w1, w2))):
                    dve.wait_ge(w_hi, 3 * g + i + 1)
                    nc.vector.tensor_tensor(w[u][1][:], src[:], w[u][0][:].bitcast(F32), ALU.subtract).then_inc(w_lo, 1)

            def low_x(g):
                for c in range(DC):
                    dve.wait_ge(x_hi, DC * g + c + 1)
                    ins = nc.vector.tensor_tensor(xT[1][:, c, :], B[c][:, 0:GS], xT[0][:, c, :].bitcast(F32), ALU.subtract)
                ins.then_inc(x_lo, 1)

            def low_h(g, f):
                dve.wait_ge(h_hi, FC * g + f + 1)
                nc.vector.tensor_tensor(hT[1][:, f, :], h[:, f % 2, :], hT[0][:, f, :].bitcast(F32), ALU.subtract).then_inc(h_lo, 1)

            def turn(g, j, u):
                for f in range(FC):
                    dve.wait_ge(sg_done, FC * g + f + 1)
                    if f >= 2:
                        dve.wait_ge(h_lo, FC * g + f - 1)
                    nc.vector.tensor_tensor(h[:, f % 2, :], B[3 + 2 * (f % 2)][:, 0:GS], sg[:, f % 2, :], ALU.mult).then_inc(h_done, 1)
                    if f:
                        low_h(g, f - 1)
                low_h(g, FC - 1)
                if not is_last(g):
                    low_x(g + 1)
                    low_w(g + 1, 1 - u)
                dve.wait_ge(f_out, 16 * GT * g)
                dve.wait_ge(marks_set, g + 1)
                for t in range(GT):
                    if t % 2 == 0:
                        dve.wait_ge(y_ps, YP * g + t // 2 + 1)
                    ins = nc.vector.tensor_scalar(y[:, t, :], B[6 + t // 2][:, (t % 2) * D:(t % 2 + 1) * D], weight[u][:, t:t + 1], None, ALU.mult)
                ins.then_inc(y_done, 1)

            low_w(0, 0)
            low_x(0)
            turns(dve, turn)


def finish(nc, R, k, fs_b, at_b, out_b):
    sb, sem = R.sb, R.sem
    fs, ao = [sb(f"fs{u}", [P, T, D]) for u in range(2)], [sb(f"ao{u}", [P, T, D]) for u in range(2)]
    g, s1, s2 = [[sb(f"{n}{u}", [P, T, D]) for u in range(2)] for n in ("g", "s1", "s2")]
    y = [sb(f"y{u}", [P, T, D]) for u in range(2)]
    in_ = [sem("in0"), sem("in1")]
    g_done, s1_done, s2_done, y_done = [sem(n) for n in ("g_done", "s1_done", "s2_done", "y_done")]
    y_out = [sem("y_out0"), sem("y_out1")]

    def flat(ap):
        return ap.rearrange("p t d -> p (t d)")

    with nc.Block() as block:

        @block.sync
        def _(sp):
            for u in range(2):
                sp.dma_start(fs[u][:], at(fs_b, u)).then_inc(in_[u], 16)
                sp.dma_start(ao[u][:], at(at_b, u)).then_inc(in_[u], 16)

            def turn(b, u, more):
                sp.wait_ge(y_done, b + 1)
                sp.dma_start(at(out_b, b), y[u][:]).then_inc(y_out[u], 16)
                if more:
                    sp.dma_start(fs[u][:], at(fs_b, b + 2)).then_inc(in_[u], 16)
                    sp.dma_start(ao[u][:], at(at_b, b + 2)).then_inc(in_[u], 16)

            with sp.Fori(0, NB // 2 - 1) as j:
                for u in range(2):
                    turn(2 * j + u, u, True)
            for u in range(2):
                turn(NB - 2 + u, u, False)
            for u in range(2):
                sp.wait_ge(y_out[u], 16 * NB // 2)

        @block.scalar
        def _(act):
            with act.Fori(0, NB // 2) as j:
                for u in range(2):
                    act.wait_ge(in_[u], 2 * 16 * (j + 1))
                    act.wait_ge(s2_done, 2 * j)
                    nc.scalar.activation(g[u][:], fs[u][:], ACT.Silu).then_inc(g_done, 1)

        @block.vector
        def _(dve):
            with dve.Fori(0, NB // 2) as j:
                for u in range(2):
                    b = 2 * j + u
                    dve.wait_ge(in_[u], 2 * 16 * (j + 1))
                    nc.vector.tensor_tensor(flat(s1[u][:]), flat(ao[u][:]), flat(col(k.xa_all, b)), ALU.add).then_inc(s1_done, 1)
                    dve.wait_ge(s1_done, b + 1)
                    dve.wait_ge(g_done, b + 1)
                    nc.vector.tensor_tensor(flat(s2[u][:]), flat(s1[u][:]), flat(g[u][:]), ALU.mult).then_inc(s2_done, 1)
                    dve.wait_ge(s2_done, b + 1)
                    dve.wait_ge(y_out[u], 16 * j)
                    nc.vector.tensor_tensor(flat(y[u][:]), flat(s2[u][:]), flat(col(k.x1_all, b)), ALU.add).then_inc(y_done, 1)


class Constants:
    pass


def constants(nc, R, k):
    k.ident, k.ones, k.upper = R.sb("ident", [P, P]), R.sb("ones", [P, P]), R.sb("upper", [P, P])
    k.landed = R.sem("landed")
    k.zeros = R.sb("zeros", [P, T * D])
    k.pad, k.token = R.sb("pad", [P, T, ROW]), R.sb("token", [P, NT], I32)
    k.logits = R.sb("logits", [P, T, NB, E0])
    k.slot_row, k.slot_share = R.sb("slot_row", [P, E0, NB * CAP // P], U32), R.sb("slot_share", [P, E0, NB * CAP // P])
    k.x1_all, k.xa_all = [R.sb(n, [P, NB, T, D]) for n in ("x1_all", "xa_all")]
    k.weight, k.slot1, k.owner = R.sb("weight", [P, TOP, NT]), R.sb("slot1", [P, NB, TOP, T], U32), R.sb("owner", [P, NG], I32)
    k.logits1 = R.sb("logits1", [P, NB, T, E1])
    k.made = made = R.sem("made")
    with nc.Block() as block:

        @block.gpsimd
        def _(pool):
            nc.gpsimd.memset(k.zeros[:], 0.0).then_inc(made, 1)
            nc.gpsimd.memset(k.ones[:], 1.0).then_inc(made, 1)
            nc.gpsimd.memset(k.ident[:], 0.0).then_inc(made, 1)
            pool.wait_ge(made, 3)
            nc.gpsimd.affine_select(out=k.ident[:], in_=k.ident[:], compare_op=ALU.not_equal, fill=1.0,
                                    base=0, pattern=[[-1, P]], channel_multiplier=1).then_inc(made, 1)
            nc.gpsimd.affine_select(out=k.upper[:], in_=k.ones[:], compare_op=ALU.is_ge, fill=0.0,
                                    base=0, pattern=[[1, P]], channel_multiplier=-1).then_inc(made, 1)
            nc.gpsimd.iota(k.token[:], pattern=[[P, NT]], base=0, channel_multiplier=1).then_inc(made, 1)
            nc.gpsimd.memset(k.pad[:], 0.0).then_inc(made, 1)
            pool.wait_ge(made, 7)
            nc.gpsimd.iota(k.pad[:].bitcast(I32)[:, :, D:D + 1], pattern=[[P, T], [0, 1]], base=NTOK, channel_multiplier=1).then_inc(made, 1)
            pool.wait_ge(made, 8)


def build(nc, a, out, phases=9):
    def scratch(name, shape, dt=F32):
        return nc.dram_tensor(name, list(shape), dt).ap()

    def tiled(ap, t=T):
        return ap.rearrange("(b t p) d -> b p t d", t=t, p=P)

    def chunked(ap):
        return ap.rearrange("(c p) f -> p c f", p=P)

    x = a["x"].rearrange("b s d -> (b s) d")
    xn0, s0, f0 = scratch("xn0", [NTOK, D]), scratch("s0", [NTOK, D]), scratch("f0", [NTOK, D])
    fs1, at1 = scratch("fs1", [NTOK + S, D]), scratch("at1", [NTOK, D])
    xn1, v1 = scratch("xn1", [NTOK, D]), scratch("v1", [NTOK, NH * 2 * HD])
    qk1 = scratch("qk1", [4 * DC, P, NTOK])
    xs = scratch("xs", [NG * GS, ROW])
    k = Constants()
    with ExitStack() as whole:
        constants(nc, Room(nc, whole, "c_"), k)
        with ExitStack() as ctx:
            layer0_mixer(nc, Room(nc, ctx, "m0_"), k, tiled(x), tiled(xn0), tiled(s0), tiled(f0), tiled(xs), at(tiled(fs1), NB), chunked(a["w_qkv"]), chunked(a["w_swiglu"]),
                         chunked(a["w_out"]), chunked(a["router_w1"]), a["router_w2"])
        if phases < 2:
            return
        with ExitStack() as ctx:
            choose_tokens(nc, Room(nc, ctx, "ct_"), k)
        with ExitStack() as ctx:
            layer0_experts(nc, Room(nc, ctx, "e0_"), k, xn0, f0, a["w1"].rearrange("e (c p) f -> e p c f", p=P),
                           a["w2"].rearrange("e (c p) f -> e p c f", p=P), a["w3"].rearrange("e (c p) f -> e p c f", p=P))
        if phases < 3:
            return
        lnw, lnb = a["ln_scale"], a["ln_bias"]
        weights = {n: chunked(a[n]) for n in ("wq", "wk", "wv", "Wr", "Ws1", "Ws3", "Ws2")}
        weights.update(lnw=lnw.rearrange("(c p) -> p c", p=P), lnb=lnb.rearrange("(c p) -> p c", p=P),
                       lnw_row=lnw.partition_broadcast(P), lnb_row=lnb.partition_broadcast(P))
        with ExitStack() as ctx:
            layer1_prepare(nc, Room(nc, ctx, "p1_"), k, tiled(x), tiled(s0), tiled(f0), tiled(xn1), tiled(v1), tiled(fs1[0:NTOK]),
                           [qk1[i].rearrange("p (b s) -> b p s", s=S) for i in range(4 * DC)], weights)
        if phases < 4:
            return
        parts = qk1.rearrange("(l a c) p n -> l a (c p) n", l=2, a=2)
        qk_v = [[[parts[l, i, q * QH * HD:(q + 1) * QH * HD].rearrange("(h d) (b s) -> b d h s", d=HD, s=S) for q in range(NQ)]
                 for i in range(2)] for l in range(2)]
        v_v = [tiled(v1[:, q * QH * 2 * HD:(q + 1) * QH * 2 * HD]) for q in range(NQ)]
        o_v = [tiled(at1[:, q * QH * HD:(q + 1) * QH * HD]) for q in range(NQ)]
        with ExitStack() as ctx:
            layer1_route(nc, Room(nc, ctx, "r1_"), k, a["rb"].partition_broadcast(P))
        with ExitStack() as ctx:
            layer1_attention(nc, Room(nc, ctx, "a1_"), k, qk_v, v_v, o_v, tiled(xn1), xs)
        if phases < 5:
            return
        with ExitStack() as ctx:
            layer1_experts(nc, Room(nc, ctx, "e1_"), k, tiled(xs), fs1, a["W1"].rearrange("e (c p) f -> e p c f", p=P),
                           a["W2"].rearrange("e (c p) f -> e p c f", p=P), a["W3"].rearrange("e (c p) f -> e p c f", p=P))
        with ExitStack() as ctx:
            finish(nc, Room(nc, ctx, "f_"), k, tiled(fs1[0:NTOK]), tiled(at1), tiled(out.rearrange("b s d -> (b s) d")))


_NAMES = ["x", "w_qkv", "w_swiglu", "w_out", "router_w1", "router_w2", "w1", "w2", "w3", "ln_scale", "ln_bias", "wq", "wk", "wv",
          "Wr", "rb", "W1", "W2", "W3", "Ws1", "Ws2", "Ws3"]


def layout(inputs):
    full = {n.split("_", 2)[2]: v for n, v in inputs.items()}
    arrays = {n: np.ascontiguousarray(full[n]) for n in _NAMES}
    for n in ("w_qkv", "w_swiglu", "w_out"):
        arrays[n] = np.ascontiguousarray(np.asarray(full[n]).T)
    return arrays


def kernel(**inputs):
    import concourse.bacc as _bacc
    from concourse.bass_utils import run_bass_kernel_spmd as _run

    nc = _bacc.Bacc("TRN2", target_bir_lowering=False, num_devices=1)
    arrays = layout(inputs)
    a = {n: nc.dram_tensor("in_" + n, v.shape, mybir.dt.from_np(v.dtype), kind="ExternalInput").ap() for n, v in arrays.items()}
    out = nc.dram_tensor("out", (NB, S, D), F32, kind="ExternalOutput").ap()
    build(nc, a, out)
    r = _run(nc, [{"in_" + n: v for n, v in arrays.items()}], core_ids=[0])
    return r.results[0]["out"]
```
